# Optimizing a Trainium2 kernel written in Bass

```python
import numpy as np
import jax
import jax.numpy as jnp

def _softmax(x, axis=-1):
    return jax.nn.softmax(x, axis=axis)

def _gelu(x):
    return jax.nn.gelu(x, approximate=True)

def _silu(x):
    return jax.nn.silu(x)

def _sigmoid(x):
    return jax.nn.sigmoid(x)

def _layernorm(x, axis=-1, eps=1e-05):
    m = jnp.mean(x, axis=axis, keepdims=True)
    v = jnp.var(x, axis=axis, keepdims=True)
    return (x - m) / jnp.sqrt(v + eps)

def _scatter_add(tgt, idx, src, axis=0):
    return tgt.at[idx].add(src)

def _segment_sum(src, seg, n):
    return jax.ops.segment_sum(src, seg, n)
kernel_name = 'mk_adaln_d1_jaxref_r8_2f0ffc'

def setup_inputs(seed: int=0):
    np.random.seed(seed)
    _w = jnp.asarray

    def _L0_attn_setup():
        import jax, jax.numpy as jnp
        import numpy as np
        D_MODEL = 128
        N_HEADS = 16
        N_KV_HEADS = 4
        HEAD_DIM = D_MODEL // N_HEADS
        N_REP = N_HEADS // N_KV_HEADS
        THETA = 10000.0
        LOGIT_CAP = 30.0
        EPS = 1e-06
        SCALE = HEAD_DIM ** (-0.5)

        def rmsnorm(x, w):
            return x * jax.lax.rsqrt(jnp.mean(x * x, axis=-1, keepdims=True) + EPS) * w

        def rope_tables(seq_len, dtype):
            inv_freq = 1.0 / THETA ** (jnp.arange(0, HEAD_DIM, 2, dtype=jnp.float32) / HEAD_DIM)
            t = jnp.arange(seq_len, dtype=jnp.float32)
            freqs = jnp.outer(t, inv_freq)
            emb = jnp.concatenate([freqs, freqs], axis=-1)
            return (jnp.cos(emb).astype(dtype), jnp.sin(emb).astype(dtype))

        def rotate_half(x):
            x1, x2 = jnp.split(x, 2, axis=-1)
            return jnp.concatenate([-x2, x1], axis=-1)

        def apply_rope(x, cos, sin):
            return x * cos + rotate_half(x) * sin
        key = jax.random.key(seed)
        ks = jax.random.split(key, 7)
        B, S = (4, 256)
        w = 0.02
        return {'x': jax.random.normal(ks[0], (B, S, D_MODEL), dtype=jnp.float32), 'Wq': jax.random.normal(ks[1], (N_HEADS * HEAD_DIM, D_MODEL), dtype=jnp.float32) * w, 'Wk': jax.random.normal(ks[2], (N_KV_HEADS * HEAD_DIM, D_MODEL), dtype=jnp.float32) * w, 'Wv': jax.random.normal(ks[3], (N_KV_HEADS * HEAD_DIM, D_MODEL), dtype=jnp.float32) * w, 'Wo': jax.random.normal(ks[4], (D_MODEL, N_HEADS * HEAD_DIM), dtype=jnp.float32) * w, 'q_norm_w': jnp.ones((HEAD_DIM,), dtype=jnp.float32), 'k_norm_w': jnp.ones((HEAD_DIM,), dtype=jnp.float32)}
    _L0_attn_in = _L0_attn_setup()

    def _L0_ffn_setup():
        import jax, jax.numpy as jnp
        import numpy as np
        HIDDEN = 128
        NUM_EXPERTS = 8
        TOP_K = 2
        B, S = (2, 256)
        key = jax.random.key(seed)
        k1, k2, k3, k4, k5 = jax.random.split(key, 5)
        d, dff, E = (HIDDEN, 4 * HIDDEN, NUM_EXPERTS)
        x = jax.random.normal(k1, (B, S, d), dtype=jnp.float32)
        W1 = jax.random.normal(k2, (E, d, dff), dtype=jnp.float32) * (1.0 / np.sqrt(d))
        b1 = jax.random.normal(k3, (E, dff), dtype=jnp.float32) * 0.01
        W2 = jax.random.normal(k4, (E, dff, d), dtype=jnp.float32) * (1.0 / np.sqrt(dff))
        b2 = jax.random.normal(k5, (E, d), dtype=jnp.float32) * 0.01
        return {'x': x, 'W1': W1, 'b1': b1, 'W2': W2, 'b2': b2}
    _L0_ffn_in = _L0_ffn_setup()
    _L0_c = _w((lambda *s: np.random.randn(*s).astype(np.float32) * 0.05)(4, 128))
    _L0_wmod = _w((lambda *s: np.random.randn(*s).astype(np.float32) * 0.05)(128, 6 * 128) * 128 ** (-0.5))
    _d = {'L0_attn_x': _L0_attn_in['x'], 'L0_attn_Wq': _L0_attn_in['Wq'], 'L0_attn_Wk': _L0_attn_in['Wk'], 'L0_attn_Wv': _L0_attn_in['Wv'], 'L0_attn_Wo': _L0_attn_in['Wo'], 'L0_attn_q_norm_w': _L0_attn_in['q_norm_w'], 'L0_attn_k_norm_w': _L0_attn_in['k_norm_w'], 'L0_ffn_W1': _L0_ffn_in['W1'], 'L0_ffn_b1': _L0_ffn_in['b1'], 'L0_ffn_W2': _L0_ffn_in['W2'], 'L0_ffn_b2': _L0_ffn_in['b2'], 'L0_c': _L0_c, 'L0_wmod': _L0_wmod}
    _x0 = _d['L0_attn_x']
    _d['L0_attn_x'] = jax.random.normal(jax.random.fold_in(jax.random.key(seed), 1), (4, 1024, 128), dtype=_x0.dtype)
    del _x0
    return _d

def reference(L0_attn_x, L0_attn_Wq, L0_attn_Wk, L0_attn_Wv, L0_attn_Wo, L0_attn_q_norm_w, L0_attn_k_norm_w, L0_ffn_W1, L0_ffn_b1, L0_ffn_W2, L0_ffn_b2, L0_c, L0_wmod):

    def _L0_attn_ref(x, Wq, Wk, Wv, Wo, q_norm_w, k_norm_w):
        import jax, jax.numpy as jnp
        import numpy as np
        D_MODEL = 128
        N_HEADS = 16
        N_KV_HEADS = 4
        HEAD_DIM = D_MODEL // N_HEADS
        N_REP = N_HEADS // N_KV_HEADS
        THETA = 10000.0
        LOGIT_CAP = 30.0
        EPS = 1e-06
        SCALE = HEAD_DIM ** (-0.5)

        def rmsnorm(x, w):
            return x * jax.lax.rsqrt(jnp.mean(x * x, axis=-1, keepdims=True) + EPS) * w

        def rope_tables(seq_len, dtype):
            inv_freq = 1.0 / THETA ** (jnp.arange(0, HEAD_DIM, 2, dtype=jnp.float32) / HEAD_DIM)
            t = jnp.arange(seq_len, dtype=jnp.float32)
            freqs = jnp.outer(t, inv_freq)
            emb = jnp.concatenate([freqs, freqs], axis=-1)
            return (jnp.cos(emb).astype(dtype), jnp.sin(emb).astype(dtype))

        def rotate_half(x):
            x1, x2 = jnp.split(x, 2, axis=-1)
            return jnp.concatenate([-x2, x1], axis=-1)

        def apply_rope(x, cos, sin):
            return x * cos + rotate_half(x) * sin
        B, S, _ = x.shape
        q = (x @ Wq.T).reshape(B, S, N_HEADS, HEAD_DIM).transpose(0, 2, 1, 3)
        k = (x @ Wk.T).reshape(B, S, N_KV_HEADS, HEAD_DIM).transpose(0, 2, 1, 3)
        v = (x @ Wv.T).reshape(B, S, N_KV_HEADS, HEAD_DIM).transpose(0, 2, 1, 3)
        q = rmsnorm(q, q_norm_w)
        k = rmsnorm(k, k_norm_w)
        cos, sin = rope_tables(S, x.dtype)
        q = apply_rope(q, cos, sin)
        k = apply_rope(k, cos, sin)
        k_exp = jnp.repeat(k, N_REP, axis=1)
        v_exp = jnp.repeat(v, N_REP, axis=1)
        scores = jnp.einsum('bhqd,bhkd->bhqk', q, k_exp) * SCALE
        scores = LOGIT_CAP * jnp.tanh(scores / LOGIT_CAP)
        causal = jnp.triu(jnp.ones((S, S), dtype=bool), k=1)
        scores = jnp.where(causal, -jnp.inf, scores)
        attn = jax.nn.softmax(scores, axis=-1)
        out = jnp.einsum('bhqk,bhkd->bhqd', attn, v_exp)
        out = out.transpose(0, 2, 1, 3).reshape(B, S, N_HEADS * HEAD_DIM)
        return out @ Wo.T

    def _L0_ffn_ref(x, W1, b1, W2, b2):
        import jax, jax.numpy as jnp
        import numpy as np
        HIDDEN = 128
        NUM_EXPERTS = 8
        TOP_K = 2
        B, S = (2, 256)
        Bm, Sm, d = x.shape
        E = W1.shape[0]
        x_flat = x.reshape(-1, d)
        h = jnp.mod(x_flat[:, :TOP_K].sum(axis=1).astype(jnp.int32), E)
        sel = jnp.stack([h, jnp.mod(h + 1, E)], axis=1)

        def step(acc, params):
            e, W1e, b1e, W2e, b2e = params
            w = jnp.any(sel == e, axis=1).astype(x.dtype) / TOP_K
            y = jnp.maximum(x_flat @ W1e + b1e, 0.0) @ W2e + b2e
            return (acc + w[:, None] * y, None)
        init = jnp.zeros_like(x_flat)
        out_flat, _ = jax.lax.scan(step, init, (jnp.arange(E), W1, b1, W2, b2))
        return out_flat.reshape(Bm, Sm, d)
    x = L0_attn_x
    mod = (_silu(L0_c) @ L0_wmod).reshape(L0_c.shape[0], 6, 1, -1)
    sa, ca, ga, sb, cb, gb = (mod[:, 0], mod[:, 1], mod[:, 2], mod[:, 3], mod[:, 4], mod[:, 5])
    ga = (2 * (ga >= 0) - 1) * jnp.maximum(jnp.abs(ga), 0.25)
    gb = (2 * (gb >= 0) - 1) * jnp.maximum(jnp.abs(gb), 0.25)
    h = _layernorm(x, axis=-1) * (1 + ca) + sa
    x = x + ga * _L0_attn_ref(h, L0_attn_Wq, L0_attn_Wk, L0_attn_Wv, L0_attn_Wo, L0_attn_q_norm_w, L0_attn_k_norm_w)
    h = _layernorm(x, axis=-1) * (1 + cb) + sb
    x = x + gb * _L0_ffn_ref(h, L0_ffn_W1, L0_ffn_b1, L0_ffn_W2, L0_ffn_b2)
    return x

_drawn_inputs = setup_inputs


def setup_inputs(seed=0):
    import zlib

    import numpy as np

    out = dict(_drawn_inputs(seed))
    spreads = {'L0_attn_q_norm_w': (1.0, 0.6), 'L0_attn_k_norm_w': (1.0, 0.6)}
    factors = {'L0_attn_Wq': 8.0,
     'L0_attn_Wk': 8.0,
     'L0_attn_Wv': 8.0,
     'L0_attn_Wo': 8.0,
     'L0_ffn_b1': 45.367,
     'L0_ffn_b2': 32.318}
    for name, (base, spread) in spreads.items():
        noise = np.random.default_rng([zlib.crc32(name.encode()), seed]).standard_normal(out[name].shape)
        drawn = base * np.exp(spread * noise) if base else spread * noise
        out[name] = jnp.asarray(drawn.astype(out[name].dtype))
    for name, factor in factors.items():
        out[name] = (out[name] * factor).astype(out[name].dtype)
    return out
```

```python
from contextlib import ExitStack

import numpy as np

import concourse.bass as bass
from concourse import mybir

ALU = mybir.AluOpType
ACT = mybir.ActivationFunctionType
F32 = mybir.dt.float32
BF16 = mybir.dt.bfloat16
I32 = mybir.dt.int32
AX = mybir.AxisListType

P = 128
NB, SEQ, D = 4, 1024, 128
NH, NKV, HD = 16, 4, 8
REP = NH // NKV
NQK = NH + NKV
NE, DFF = 8, 512
NC = DFF // P
QB = 512
TU = QB // P
TB = SEQ // P
NPIECE = 3
KR = NPIECE * NPIECE * HD
CAP = 30.0
SCALE = float(HD) ** -0.5
LN_EPS, RMS_EPS = 1e-5, 1e-6
QKVW = (NH + 2 * NKV) * HD
VW = 32
RING = 4

KB_OF = (TU, 2 * TU)
SLOTS_OF = (NKV * KB_OF[0], NKV * KB_OF[1])
SLOTS = sum(SLOTS_OF)
assert SLOTS % RING == 0 and SLOTS_OF[0] % RING == 0

SETUP_USES = 1 + NB
PREP = [("ln1",), ("xn", 0), ("lnT", 0), ("xn", 1), ("lnT", 1), ("qkv", 0), ("qkv", 1), ("rms", 0), ("qkv", 2),
        ("qT", 0), ("kT", 0), ("qkv", 3), ("rms", 1), ("qT", 1), ("kT", 1)]
NO_BANK = {"ln1", "xn", "rms", "end", "v0", "v1"}


def plan(qb, before, prep):
    nkb, n = KB_OF[qb], SLOTS_OF[qb]
    at = [[] for _ in range(n)]
    for k in range(NKV - 1):
        at[(k + 1) * nkb + 1].append(("turn", k))
    if before:
        first = 6
        at[1].append(("turn", NKV - 1))
        at[2].append(("oT",))
        at[3].append(("wo",))
        at[5] += [("ln2",), ("w8",)]
        at[6].append(("b2",))
        for u in range(NE * NC):
            at[first + u * (n - first) // (NE * NC)].append(("ffn", u))
        at[n - 1].append(("end",))
    if prep:
        for i, item in enumerate(PREP):
            at[7 + i * 18 // len(PREP)].insert(0, item)
        at[27].append(("v0",))
    if before and qb == 0:
        at[2].append(("v1",))
    return at


PLAN_FIRST = plan(0, False, False)
PLAN_ODD = plan(1, True, True)
PLAN_EVEN = plan(0, True, False)
PLAN_LAST = plan(1, True, False)
PLAN_TAIL = [[("turn", NKV - 1), ("oT",), ("wo",), ("ln2",), ("w8",), ("b2",)] + [("ffn", u) for u in range(NE * NC)] + [("end",)]]


def uses(items):
    return sum(i[0] not in NO_BANK for i in items)


def uses_of(p):
    return sum(uses(s) for s in p)


USES_FIRST = SETUP_USES + uses(PREP)
USES_LOOP = uses_of(PLAN_ODD) + uses_of(PLAN_EVEN)
assert USES_LOOP % 2 == 0


def slot_base(b, qb):
    return b * SLOTS + qb * SLOTS_OF[0]


def slot_shape(qb, l):
    kv, kb = divmod(l, KB_OF[qb])
    d = kb - TU * qb
    return kv, kb, max(d, 0) * P, d >= 0


def diagonals(qb, l):
    return sum(slot_shape(qb, i)[3] for i in range(l))


def spread(ap, axis, n):
    shape = list(ap.shape)
    assert shape[axis] == 1
    shape[axis] = n
    return ap.broadcast_to(tuple(shape))


def wait(eng, sem, value):
    if isinstance(value, int) and value <= 0:
        return
    eng.wait_ge(sem, value)


CHAIN_LOOP = 141


def adaln_block(nc, x, wqkv, wo, q_w, k_w, w1, b1, w2, b2, c, wmod, rope, out, chain_counts):
    ctx = ExitStack()
    with ctx:
        def sb(name, shape, dt=F32):
            return ctx.enter_context(nc.sbuf_tensor(name, shape, dt))

        def ps(name, shape, dt=F32):
            return ctx.enter_context(nc.psum_tensor(name, shape, dt))

        def sem(name):
            return ctx.enter_context(nc.semaphore(name))

        x_all = sb("x_all", [P, NB * TB, D])
        w1_sb = sb("w1_sb", [P, NE, DFF])
        w2_sb = sb("w2_sb", [P, NE, NC, D])
        b1_sb = sb("b1_sb", [P, NE * NC])
        b2_sb = sb("b2_sb", [NE, D])
        wqkv_t = sb("wqkv_t", [P, QKVW])
        wo_t = sb("wo_t", [P, D])
        c_t = sb("c_t", [P, NB])
        silu_w = sb("silu_w", [P, 3, NB])
        mod_t = sb("mod_t", [P, 6, NB])
        mod_bc = sb("mod_bc", [P, NB, 4 * D])
        ident = sb("ident", [P, P])
        expert = sb("expert", [P, TU, NE], I32)
        rope_sb = sb("rope_sb", [P, 2, TB, HD])
        qk_w = sb("qk_w", [P, 2, HD])
        rope_c = sb("rope_c", [P, TB, NQK, HD])
        rope_s = sb("rope_s", [P, TB, NQK, HD])
        Q = [sb(f"q_stack{i}", [KR, NH, QB], BF16) for i in range(2)]
        K = [sb(f"k_stack{i}", [KR, NKV, KB_OF[i] * P], BF16) for i in range(2)]
        V = [sb(f"v_pad{i}", [P, KB_OF[i], NKV, VW]) for i in range(2)]
        probs = sb("probs", [P, RING, REP, QB])
        early = probs[:, RING - 1, :, :].rearrange("p h q -> p (h q)")
        wmod_sb = early[:, 3 * D:9 * D]
        gate_w = early[:, 9 * D:11 * D].rearrange("p (i d) -> p i d", i=2)
        rope_w = early[:, 11 * D:13 * D].rearrange("p (f n t d) -> p f n t d", f=2, n=2, t=TB)
        silu_bc = probs[:, RING - 2, 0, :].rearrange("p (b c) -> p b c", b=NB)
        stats = sb("stats", [P, TB, 6])
        mean_var = sb("mean_var", [P, TB, 2])
        rstd = sb("rstd", [P, TB])
        nw_a = sb("nw_a", [P, TU * NQK])
        nw_i = sb("nw_i", [P, TU * NQK], I32)
        var_e = sb("var_e", [P, TU * NQK])
        rms = sb("rms", [P, TU * NQK])
        xn = sb("xn", [P, TU, D])
        h_t = sb("h_t", [P, SEQ])
        qkv = sb("qkv", [P, TB, QKVW])
        rot_a = sb("rot_a", [P, TU, NQK * HD])
        rot_b = sb("rot_b", [P, TU, NQK * HD])
        k_rot = sb("k_rot", [P, TU, NKV * HD])
        rest = sb("rest", [P, QB])
        q_pieces = sb("q_pieces", [P, NPIECE, SEQ], BF16)
        k_pieces = sb("k_pieces", [P, NPIECE, 2, P], BF16)
        o_sb = sb("o_sb", [P, 2, QB])
        den = sb("den", [P, TU, REP])
        o_tok = sb("o_tok", [P, TU, D])
        o_t = sb("o_t", [P, QB])
        x2 = sb("x2", [P, 2, TU, D])
        xn2 = sb("xn2", [P, TU, D])
        stats2 = sb("stats2", [P, TU, 6])
        mean_var2 = sb("mean_var2", [P, TU, 2])
        rstd2 = sb("rstd2", [P, TU])
        h2_t = sb("h2_t", [P, QB])
        pick = sb("pick", [P, TU, 2])
        pick_f = sb("pick_f", [P, 5, TU])
        pick_i = sb("pick_i", [P, 2, TU], I32)
        near = sb("near", [P, TU, NE], I32)
        w8 = sb("w8", [P, TU, NE])
        w8_t = sb("w8_t", [NE, QB])
        h1 = sb("h1", [P, 2, QB])
        acc = sb("acc", [P, TU, D])

        scores = ps("scores", [P, REP, QB])
        o_ps = ps("o_ps", [P, QB])
        bank = ps("bank", [P, 2, QB])
        y_ps = ps("y_ps", [P, TU, D])

        scratch = nc.dram_tensor("scratch", (NB, NPIECE, (NH + NKV) * HD, SEQ), BF16, kind="Internal").ap()

        s_alone = sem("s_alone")
        s_small = sem("s_small")
        s_x0 = sem("s_x0")
        s_x = sem("s_x")
        s_rope_in = sem("s_rope_in")
        s_ffn_in = sem("s_ffn_in")
        s_const = sem("s_const")
        s_tables = sem("s_tables")
        s_exp0 = sem("s_exp0")
        s_silu = sem("s_silu")
        s_xn = sem("s_xn")
        s_chain = sem("s_chain")
        s_bank_full = sem("s_bank_full")
        s_bank_free = sem("s_bank_free")
        s_roped = sem("s_roped")
        s_split = sem("s_split")
        s_stored = sem("s_stored")
        s_stack = [sem("s_stack0"), sem("s_stack1")]
        s_v = [sem("s_v0"), sem("s_v1")]
        s_scored = sem("s_scored")
        s_tanh = sem("s_tanh")
        s_exp = sem("s_exp")
        s_masked = sem("s_masked")
        s_pv = sem("s_pv")
        s_o = sem("s_o")
        s_xn2 = sem("s_xn2")
        s_w8 = sem("s_w8")
        s_h1_used = sem("s_h1_used")
        s_y = sem("s_y")
        s_y_free = sem("s_y_free")
        s_out = sem("s_out")
        s_x2_free = [sem("s_x2_free0"), sem("s_x2_free1")]

        def ds(i, n):
            return slice(i, i + n) if isinstance(i, int) else bass.ds(i, n)

        def use_base(where, b):
            if where == "first":
                return USES_FIRST
            base = USES_FIRST + uses_of(PLAN_FIRST) + b * USES_LOOP
            if where == "even":
                return base + uses_of(PLAN_ODD)
            if where == "tail":
                return base + uses_of(PLAN_LAST)
            return base

        use_parity = {w: (use_base(w, 0)) % 2 for w in ("first", "odd", "even", "last")}
        use_parity["tail"] = use_base("tail", NB - 1) % 2
        STORES = 1 + TU * NPIECE
        LOADS = NPIECE * NPIECE * 2

        block = ctx.enter_context(nc.Block())

        @block.sync
        def _(sp):
            sp.dma_start(c_t[:, :], c).then_inc(s_small, 16)
            sp.dma_start(wmod_sb[:, :], wmod).then_inc(s_small, 16)
            sp.dma_start(wqkv_t[:, :], wqkv).then_inc(s_small, 16)
            sp.dma_start(wo_t[:, :], wo).then_inc(s_small, 16)
            xt = x.rearrange("b (t p) d -> p (b t) d", p=P)
            sp.dma_start(x_all[:, 0:TB, :], xt[:, 0:TB, :]).then_inc(s_x0, 16)
            sp.dma_start(rope_sb[:, :, :, :], rope.rearrange("f (t p) d -> p f t d", p=P)).then_inc(s_rope_in, 16)
            sp.dma_start(qk_w[:, 0, :], spread(q_w.rearrange("(a d) -> a d", a=1), 0, P)).then_inc(s_rope_in, 16)
            sp.dma_start(qk_w[:, 1, :], spread(k_w.rearrange("(a d) -> a d", a=1), 0, P)).then_inc(s_rope_in, 16)
            sp.dma_start(x_all[:, TB:, :], xt[:, TB:, :]).then_inc(s_x, 16)
            sp.dma_start(w1_sb[:, :, :], w1.rearrange("e d f -> d e f")).then_inc(s_ffn_in, 16)
            sp.dma_start(w2_sb[:, :, :, :], w2.rearrange("e (c p) d -> p e c d", p=P)).then_inc(s_ffn_in, 16)
            sp.dma_start(b1_sb[:, :], b1).then_inc(s_ffn_in, 16)
            sp.dma_start(b2_sb[:, :], b2).then_inc(s_ffn_in, 16)

            def store_pieces(b):
                sp.wait_ge(s_split, 4 * b + 4)
                sp.dma_start(scratch[ds(b, 1), :, 0:NH * HD, :].rearrange("a i r t -> r (a i) t"),
                             q_pieces[:, :, :]).then_inc(s_stored, 16)
                for l in range(TU):
                    for i in range(NPIECE):
                        dst = scratch[ds(b, 1), i, NH * HD:, :].rearrange("a r (h l c) -> (a r) h l c", h=2, c=P)
                        sp.dma_start(dst[:, :, l, :], k_pieces[32 * l:32 * l + 32, i, :, :]).then_inc(s_stored, 16)

            def load_stacks(b, qb):
                if qb == 0:
                    sp.wait_ge(s_stored, 16 * STORES * (b + 1))
                wait(sp, s_scored, 2 * (slot_base(b, 0) if qb else slot_base(b - 1, 1)))
                for i in range(NPIECE):
                    for j in range(NPIECE):
                        r = (i * NPIECE + j) * HD
                        src = scratch[ds(b, 1), i, 0:NH * HD, qb * QB:(qb + 1) * QB].rearrange("a (h d) t -> d (a h) t", d=HD)
                        sp.dma_start(Q[qb][r:r + HD, :, :], src).then_inc(s_stack[qb], 16)
                        src = scratch[ds(b, 1), j, NH * HD:, 0:KB_OF[qb] * P].rearrange("a (h d) t -> d (a h) t", d=HD)
                        sp.dma_start(K[qb][r:r + HD, :, :], src).then_inc(s_stack[qb], 16)

            def store_out(b, qb):
                sp.wait_ge(s_out, 2 * b + qb + 1)
                sp.dma_start(xo[:, ds(b * TB + qb * TU, TU), :], x2[:, qb, :, :]).then_inc(s_x2_free[qb], 16)

            xo = out.rearrange("b (t p) d -> p (b t) d", p=P)
            store_pieces(0)
            load_stacks(0, 0)
            load_stacks(0, 1)
            with sp.Fori(0, NB - 1) as b:
                store_pieces(b + 1)
                load_stacks(b + 1, 0)
                store_out(b, 0)
                load_stacks(b + 1, 1)
                store_out(b, 1)
            store_out(NB - 1, 0)
            store_out(NB - 1, 1)
            for qb in range(2):
                sp.wait_ge(s_x2_free[qb], 16 * (NB + 1))

        @block.gpsimd
        def _(pool):
            own = [0]

            def done(ins):
                own[0] += 1
                ins.then_inc(s_const, 1)

            done(nc.gpsimd.memset(ident[:, :], 0.0))
            done(nc.gpsimd.iota(expert[:, :, :], pattern=[[0, TU], [1, NE]], base=0, channel_multiplier=0))
            for v in V:
                done(nc.gpsimd.memset(v[:, :, :, :], 0.0))
            pool.wait_ge(s_const, own[0])
            done(nc.gpsimd.affine_select(out=ident[:, :], in_=ident[:, :], compare_op=ALU.not_equal, fill=1.0, base=0,
                                         pattern=[[-1, P]], channel_multiplier=1))
            for v in V:
                done(nc.gpsimd.memset(v[:, :, :, HD:HD + 1], 1.0))
            pool.wait_ge(s_const, own[0])
            pool.wait_ge(s_rope_in, 48)
            for n in range(2):
                w = spread(qk_w[:, n:n + 1, :], 1, TB)
                nc.gpsimd.tensor_tensor(rope_w[:, 0, n, :, :], rope_sb[:, 0, :, :], w, ALU.mult).then_inc(s_tables, 1)
                for half in range(2):
                    here = slice(half * HD // 2, (half + 1) * HD // 2)
                    there = slice((1 - half) * HD // 2, (2 - half) * HD // 2)
                    nc.gpsimd.tensor_tensor(rope_w[:, 1, n, :, here], rope_sb[:, 1, :, here],
                                            w[:, :, there], ALU.mult).then_inc(s_tables, 1)
            pool.wait_ge(s_tables, 6)
            for f, table in enumerate((rope_c, rope_s)):
                for n, (h0, h1_) in enumerate(((0, NH), (NH, NQK))):
                    src = spread(rope_w[:, f, n, :, :].rearrange("p t (a d) -> p t a d", a=1), 2, h1_ - h0)
                    nc.gpsimd.tensor_copy(table[:, :, h0:h1_, :], src).then_inc(s_tables, 1)

            def pad_values(b, qb):
                pool.wait_ge(s_roped, 2 * b + 2)
                wait(pool, s_pv, slot_base(b, 0) if qb else slot_base(b - 1, 1))
                pool.sem_inc(s_alone, 1)
                src = qkv[:, 0:KB_OF[qb], NQK * HD:].rearrange("p t (k d) -> p t k d", d=HD)
                nc.gpsimd.tensor_copy(V[qb][:, :, :, 0:HD], src).then_inc(s_v[qb], 1)

            def phase(b, qb, items):
                for l in range(SLOTS_OF[qb]):
                    g = slot_base(b, qb) + l
                    kv, kb, off, diagonal = slot_shape(qb, l)
                    if diagonal:
                        pool.wait_ge(s_exp, g + 1)
                        pool.sem_inc(s_alone, 1)
                        tri = probs[:, l % RING, :, off:off + P]
                        nc.gpsimd.affine_select(out=tri, in_=tri, compare_op=ALU.is_ge, fill=0.0, base=0,
                                                pattern=[[0, REP], [1, P]], channel_multiplier=-1).then_inc(s_masked, 1)
                    for item in items[l]:
                        if item[0] == "v0":
                            pad_values(b + 1, 0)
                        if item[0] == "v1":
                            pad_values(b, 1)

            pad_values(0, 0)
            pad_values(0, 1)
            phase(0, 0, PLAN_FIRST)
            with pool.Fori(0, NB - 1) as b:
                phase(b, 1, PLAN_ODD)
                phase(b + 1, 0, PLAN_EVEN)
            phase(NB - 1, 1, PLAN_LAST)

        @block.scalar
        def _(act):
            act.wait_ge(s_small, 16 * 4)
            nc.scalar.activation(silu_w[:, 0, :], c_t[:, :], ACT.Exp, scale=-1.0).then_inc(s_exp0, 1)

            def cap(b, qb, l):
                g = slot_base(b, qb) + l
                _, _, off, _ = slot_shape(qb, l)
                r = l % RING
                wait(act, s_pv, g - RING + 1)
                if off < QB // 2:
                    for pair in range(2):
                        act.wait_ge(s_scored, 2 * g + pair + 1)
                        h = slice(2 * pair, 2 * pair + 2)
                        nc.scalar.activation(probs[:, r, h, off:QB], scores[:, h, off:QB], ACT.Tanh,
                                             scale=SCALE / CAP).then_inc(s_tanh, 1)
                else:
                    act.wait_ge(s_scored, 2 * g + 2)
                    nc.scalar.activation(probs[:, r, :, off:QB], scores[:, :, off:QB], ACT.Tanh,
                                         scale=SCALE / CAP).then_inc(s_tanh, 2)

            def exponential(b, qb, l):
                g = slot_base(b, qb) + l
                _, _, off, _ = slot_shape(qb, l)
                p = probs[:, l % RING, :, off:QB]
                act.wait_ge(s_tanh, 2 * g + 2)
                nc.scalar.activation(p, p, ACT.Exp, scale=CAP).then_inc(s_exp, 1)

            def phase(b, qb, last=False):
                n = SLOTS_OF[qb]
                for l in range(n):
                    if l + 1 < n:
                        cap(b, qb, l + 1)
                    elif not last:
                        cap(b + qb, 1 - qb, 0)
                    exponential(b, qb, l)

            cap(0, 0, 0)
            phase(0, 0)
            with act.Fori(0, NB - 1) as b:
                phase(b, 1)
                phase(b + 1, 0)
            phase(NB - 1, 1, last=True)

        @block.tensor
        def _(pe):
            use = {}

            def begin(where, b):
                use["base"], use["n"], use["parity"] = use_base(where, b), 0, use_parity[where]

            def take():
                n = use["base"] + use["n"]
                wait(pe, s_bank_free, n - 1)
                p = bank[:, (use["parity"] + use["n"]) % 2, :]
                use["n"] += 1
                return p, n

            def read_of(n):
                pe.wait_ge(s_bank_free, n + 1)

            def transposes(p, src_of, rows=P):
                for t in range(TU):
                    last = nc.tensor.transpose(p[0:rows, t * P:(t + 1) * P], src_of(t), ident[:, :])
                last.then_inc(s_bank_full, 1)

            use.update(base=0, n=0, parity=0)
            pe.wait_ge(s_small, 16 * 4)
            pe.wait_ge(s_const, 7)
            pe.wait_ge(s_silu, 1)
            p, _ = take()
            for i in range(6):
                last = nc.tensor.matmul(p[:, i * NB:(i + 1) * NB], wmod_sb[:, i * D:(i + 1) * D], silu_w[:, 2, :],
                                        start=True, stop=True)
            last.then_inc(s_bank_full, 1)
            pe.wait_ge(s_silu, 2)
            for b in range(NB):
                p, _ = take()
                nc.tensor.matmul(p[:, :], silu_bc[:, b, :], wmod_sb[:, 2 * D:], start=True, stop=True).then_inc(s_bank_full, 1)

            def prep(item, b, marks):
                kind, k = item
                if kind == "lnT":
                    pe.wait_ge(s_xn, 2 * b + k + 1)
                    p, n = take()
                    transposes(p, lambda t: xn[:, t, :])
                    marks[item] = n
                if kind == "qkv":
                    p, n = take()
                    read_of(marks["lnT", k // 2])
                    for t in range(2):
                        i = 2 * k + t
                        last = nc.tensor.matmul(p[:, t * QKVW:(t + 1) * QKVW], h_t[:, i * P:(i + 1) * P], wqkv_t[:, :],
                                                start=True, stop=True)
                    last.then_inc(s_bank_full, 1)
                if kind == "qT":
                    p, n = take()
                    pe.wait_ge(s_roped, 2 * b + k + 1)
                    transposes(p, lambda t: rot_b[:, t, 0:NH * HD])
                if kind == "kT":
                    p, n = take()
                    pe.wait_ge(s_roped, 2 * b + k + 1)
                    nc.tensor.transpose(p[:, 0:P], k_rot[:, :, :].rearrange("p t d -> p (t d)"), ident[:, :]).then_inc(s_bank_full, 1)

            def qk(b, qb, l):
                g = slot_base(b, qb) + l
                kv, kb, off, _ = slot_shape(qb, l)
                if l == 0:
                    pe.wait_ge(s_stack[qb], 16 * LOADS * (b + 1))
                for hh in range(REP):
                    if hh % 2 == 0:
                        wait(pe, s_tanh, 2 * (g - 1) + hh // 2 + 1)
                    last = nc.tensor.matmul(scores[:, hh, off:QB], K[qb][:, kv, kb * P:(kb + 1) * P],
                                            Q[qb][:, kv * REP + hh, off:QB], start=True, stop=True)
                    if hh % 2:
                        last.then_inc(s_scored, 1)

            def pv(b, qb, l):
                g = slot_base(b, qb) + l
                kv, kb, off, diagonal = slot_shape(qb, l)
                if l == 0:
                    pe.wait_ge(s_v[qb], b + 1)
                if kb == 0:
                    wait(pe, s_o, b * 2 * NKV + qb * NKV + kv)
                if diagonal:
                    pe.wait_ge(s_masked, b * 2 * NKV * TU + diagonals(0, qb * SLOTS_OF[0]) + diagonals(qb, l) + 1)
                else:
                    pe.wait_ge(s_exp, g + 1)
                for hh in range(REP):
                    last = nc.tensor.matmul(o_ps[32 * hh:32 * hh + VW, off:QB], V[qb][:, kb, kv, :],
                                            probs[:, l % RING, hh, off:QB], start=(kb == 0),
                                            stop=(kb == KB_OF[qb] - 1))
                last.then_inc(s_pv, 1)

            def finish(item, b, qb, own_b, own_qb, marks):
                kind = item[0]
                unit = 2 * b + qb
                if kind == "turn":
                    k = item[1]
                    ub, uqb = (b, qb) if k == NKV - 1 else (own_b, own_qb)
                    pe.wait_ge(s_o, ub * 2 * NKV + uqb * NKV + k + 1)
                    p, n = take()
                    transposes(p, lambda t: o_sb[:, k % 2, t * P:(t + 1) * P])
                    marks[kind] = n
                if kind == "oT":
                    read_of(marks["turn"])
                    p, n = take()
                    transposes(p, lambda t: o_tok[:, t, :])
                    marks[kind] = n
                if kind == "wo":
                    read_of(marks["oT"])
                    p, n = take()
                    for t in range(TU):
                        last = nc.tensor.matmul(p[:, t * D:(t + 1) * D], o_t[:, t * P:(t + 1) * P], wo_t[:, :],
                                                start=True, stop=True)
                    last.then_inc(s_bank_full, 1)
                if kind == "ln2":
                    pe.wait_ge(s_xn2, unit + 1)
                    p, n = take()
                    transposes(p, lambda t: xn2[:, t, :])
                    marks[kind] = n
                if kind == "w8":
                    pe.wait_ge(s_w8, unit + 1)
                    p, n = take()
                    transposes(p, lambda t: w8[:, t, :], rows=NE)
                    marks[kind] = n
                if kind == "b2":
                    read_of(marks["w8"])
                    p, n = take()
                    for t in range(TU):
                        last = nc.tensor.matmul(p[:, t * D:(t + 1) * D], w8_t[:, t * P:(t + 1) * P], b2_sb[:, :],
                                                start=True, stop=True)
                    last.then_inc(s_bank_full, 1)
                if kind == "ffn":
                    e, ch = divmod(item[1], NC)
                    if item[1] == 0:
                        read_of(marks["ln2"])
                    p, n = take()
                    nc.tensor.matmul(p[:, :], w1_sb[:, e, ch * P:(ch + 1) * P], h2_t[:, :],
                                     start=True, stop=True).then_inc(s_bank_full, 1)
                    if item[1]:
                        second(item[1] - 1, unit, marks["ffn"])
                    marks["ffn"] = n
                if kind == "end":
                    second(NE * NC - 1, unit, marks["ffn"])

            def second(u, unit, n):
                e, ch = divmod(u, NC)
                read_of(n)
                if ch == 0 and e:
                    pe.wait_ge(s_y_free, NE * unit + e)
                for t in range(TU):
                    last = nc.tensor.matmul(y_ps[:, t, :], h1[:, u % 2, t * P:(t + 1) * P], w2_sb[:, e, ch, :],
                                            start=(ch == 0 and t == 0), stop=(ch == NC - 1 and t == TU - 1),
                                            skip_group_check=True)
                last.then_inc(s_h1_used, 1)

            def phase(b, qb, where, items, last=False):
                begin(where, b - (where == "even") if where != "first" else 0)
                n, marks = SLOTS_OF[qb], {}
                before = (b, 0) if qb else (b - 1, 1)
                for l in range(n):
                    if l + 1 < n:
                        qk(b, qb, l + 1)
                    elif not last:
                        qk(b + qb, 1 - qb, 0)
                    if l:
                        pv(b, qb, l - 1)
                    elif where != "first":
                        pv(*before, SLOTS_OF[before[1]] - 1)
                    for item in items[l]:
                        if item in PREP:
                            if item[0] not in NO_BANK:
                                prep(item, b + 1, marks)
                        else:
                            finish(item, *before, b, qb, marks)

            marks = {}
            for item in PREP:
                if item[0] not in NO_BANK:
                    prep(item, 0, marks)
            assert use["n"] == USES_FIRST
            qk(0, 0, 0)
            phase(0, 0, "first", PLAN_FIRST)
            pe.wait_ge(s_ffn_in, 64)
            with pe.Fori(0, NB - 1) as b:
                phase(b, 1, "odd", PLAN_ODD)
                phase(b + 1, 0, "even", PLAN_EVEN)
            phase(NB - 1, 1, "last", PLAN_LAST, last=True)
            pv(NB - 1, 1, SLOTS_OF[1] - 1)
            begin("tail", NB - 1)
            marks = {}
            for item in PLAN_TAIL[0]:
                finish(item, NB - 1, 1, NB - 1, 1, marks)

        @block.vector
        def _(dve):
            v = nc.vector
            use, chain = {}, dict(base=0, n=0)

            def link(ins, plain=False):
                chain["n"] += 1
                ins.then_inc(s_chain, 1)
                dve.wait_ge(s_chain, chain["base"] + chain["n"])
                if plain:
                    dve.sem_inc(s_alone, 1)

            def begin(where, b):
                use["base"], use["n"], use["parity"] = use_base(where, b), 0, use_parity[where]

            def full():
                dve.wait_ge(s_bank_full, use["base"] + use["n"] + 1)
                p = bank[:, (use["parity"] + use["n"]) % 2, :]
                use["n"] += 1
                return p

            def rsqrt(y, val, n):
                a, i = nw_a[:, 0:n], nw_i[:, 0:n]
                link(v.tensor_scalar(i, val.bitcast(I32), 1, None, ALU.logical_shift_right))
                link(v.tensor_scalar(y.bitcast(I32), i, -1.0, float(0x5F3759DF), ALU.mult, ALU.add))
                for _ in range(4):
                    link(v.scalar_tensor_tensor(out=a, in0=y, scalar=-0.5, in1=y, op0=ALU.mult, op1=ALU.mult))
                    link(v.tensor_tensor(a, a, val, ALU.mult))
                    link(v.scalar_tensor_tensor(out=y, in0=a, scalar=1.5, in1=y, op0=ALU.add, op1=ALU.mult))

            use.update(base=0, n=0, parity=0)
            for qb in range(2):
                v.memset(x2[:, qb, 0, 0:1], 0.0).then_inc(s_x2_free[qb], 16)
            dve.wait_ge(s_exp0, 1)
            link(v.tensor_scalar(silu_w[:, 1, :], silu_w[:, 0, :], 1.0, None, ALU.add))
            link(v.reciprocal(silu_w[:, 1, :], silu_w[:, 1, :]))
            v.tensor_tensor(silu_w[:, 2, :], c_t[:, :], silu_w[:, 1, :], ALU.mult).then_inc(s_silu, 1)
            dve.wait_ge(s_silu, 1)
            v.tensor_copy(silu_bc[:, :, :], spread(silu_w[:, 2, :].rearrange("p (b a) -> p b a", a=1), 2, P)).then_inc(s_silu, 1)
            p = full()
            link(v.tensor_copy(mod_t[:, :, :], p[:, 0:6 * NB].rearrange("p (i b) -> p i b", b=NB)))
            for i in (1, 4):
                link(v.tensor_scalar(mod_t[:, i, :], mod_t[:, i, :], 1.0, None, ALU.add))
            v.tensor_copy(nw_a[:, 0:1], mod_t[:, 0, 0:1]).then_inc(s_bank_free, 1)
            for b in range(NB):
                p = full()
                v.tensor_copy(mod_bc[:, b, :], p[:, :]).then_inc(s_bank_free, 1)
                dve.wait_ge(s_bank_free, 1 + b + 1)
                for i in (0, 3):
                    g = mod_bc[:, b, i * D:(i + 1) * D]
                    link(v.tensor_scalar(gate_w[:, 0, :], g, 0.0, 2.0, ALU.is_ge, ALU.mult))
                    link(v.tensor_scalar(gate_w[:, 1, :], g, -1.0, None, ALU.mult))
                    link(v.tensor_tensor(gate_w[:, 1, :], gate_w[:, 1, :], g, ALU.max))
                    link(v.tensor_scalar(gate_w[:, 1, :], gate_w[:, 1, :], 0.25, None, ALU.max))
                    link(v.scalar_tensor_tensor(out=g, in0=gate_w[:, 0, :], scalar=-1.0, in1=gate_w[:, 1, :],
                                                op0=ALU.add, op1=ALU.mult))
                link(v.tensor_scalar(mod_bc[:, b, 2 * D:3 * D], mod_bc[:, b, 2 * D:3 * D], 1.0, None, ALU.add))

            def prep(item, b):
                kind = item[0]
                if kind == "ln1":
                    for t in range(TB):
                        last = v.bn_stats(stats[:, t, :], x_all[:, ds(b * TB + t, 1), :])
                    link(last, plain=True)
                    for t in range(TB):
                        last = v.bn_aggr(mean_var[:, t, :], stats[:, t, :])
                    link(last)
                    link(v.tensor_scalar(var_e[:, 0:TB], mean_var[:, :, 1], LN_EPS, None, ALU.add))
                    rsqrt(rstd[:, :], var_e[:, 0:TB], TB)
                if kind == "xn":
                    k = item[1]
                    for t in range(TU):
                        i = k * TU + t
                        last = v.tensor_scalar(xn[:, t, :], x_all[:, ds(b * TB + i, 1), :], mean_var[:, i, 0:1],
                                               rstd[:, i:i + 1], ALU.subtract, ALU.mult)
                    last.then_inc(s_xn, 1)
                if kind == "lnT":
                    k, p = item[1], full()
                    v.tensor_scalar(h_t[:, k * QB:(k + 1) * QB], p, mod_t[:, 1, ds(b, 1)], mod_t[:, 0, ds(b, 1)],
                                    ALU.mult, ALU.add).then_inc(s_bank_free, 1)
                if kind == "qkv":
                    k, p = item[1], full()
                    if k == 0:
                        wait(dve, s_v[1], b)
                    v.tensor_copy(qkv[:, 2 * k:2 * k + 2, :], p[:, 0:2 * QKVW].rearrange("p (t n) -> p t n", t=2)) \
                        .then_inc(s_bank_free, 1)
                    dve.wait_ge(s_bank_free, use["base"] + use["n"])
                if kind == "rms":
                    k = item[1]
                    part = qkv[:, k * TU:(k + 1) * TU, 0:NQK * HD]
                    link(v.tensor_tensor(rot_a[:, :, :], part, part, ALU.mult))
                    ms = var_e[:, :]
                    link(v.tensor_reduce(ms, rot_a[:, :, :].rearrange("p t (h d) -> p (t h) d", d=HD), AX.X, ALU.add))
                    link(v.tensor_scalar(ms, ms, 1.0 / HD, RMS_EPS, ALU.mult, ALU.add))
                    rsqrt(rms[:, :], ms, TU * NQK)
                    if isinstance(b, int) and k == 0:
                        dve.wait_ge(s_tables, 10)
                    heads = part.rearrange("p t (h d) -> p t h d", d=HD)
                    r = spread(rms[:, :].rearrange("p (t h a) -> p t h a", t=TU, a=1), 3, HD)
                    link(v.tensor_tensor(rot_a[:, :, :].rearrange("p t (h d) -> p t h d", d=HD), heads, r, ALU.mult))
                    ra = rot_a[:, :, :].rearrange("p t (h d) -> p t h d", d=HD)
                    rb = rot_b[:, :, :].rearrange("p t (h d) -> p t h d", d=HD)
                    tiles = slice(k * TU, (k + 1) * TU)
                    half = HD // 2
                    v.tensor_tensor(rb[:, :, :, 0:half], ra[:, :, :, half:], rope_s[:, tiles, :, 0:half], ALU.mult)
                    link(v.tensor_tensor(rb[:, :, :, half:], ra[:, :, :, 0:half], rope_s[:, tiles, :, half:], ALU.mult))
                    link(v.tensor_tensor(ra, ra, rope_c[:, tiles, :, :], ALU.mult))
                    heads_q, heads_k = slice(0, NH * HD), slice(NH * HD, NQK * HD)
                    v.tensor_tensor(rot_b[:, :, heads_q], rot_b[:, :, heads_q], rot_a[:, :, heads_q], ALU.add)
                    v.tensor_tensor(k_rot[:, :, :], rot_b[:, :, heads_k], rot_a[:, :, heads_k], ALU.add).then_inc(s_roped, 1)
                if kind in ("qT", "kT"):
                    k, p = item[1], full()
                    if kind == "qT":
                        to, n = [q_pieces[:, i, k * QB:(k + 1) * QB] for i in range(NPIECE)], QB
                    else:
                        to, n = [k_pieces[:, i, k, :] for i in range(NPIECE)], P
                    if kind == "qT" and k == 0:
                        wait(dve, s_stored, 16 * STORES * b)
                    p = p[:, 0:n]
                    link(v.tensor_copy(to[0], p))
                    v.tensor_tensor(rest[:, 0:n], p, to[0], ALU.subtract).then_inc(s_bank_free, 1)
                    dve.wait_ge(s_bank_free, use["base"] + use["n"])
                    link(v.tensor_copy(to[1], rest[:, 0:n]))
                    v.tensor_tensor(to[2], rest[:, 0:n], to[1], ALU.subtract).then_inc(s_split, 1)

            def evacuate(b, qb, k):
                g = slot_base(b, qb) + (k + 1) * KB_OF[qb]
                dve.wait_ge(s_pv, g)
                v.tensor_copy(o_sb[:, k % 2, :], o_ps[:, :]).then_inc(s_o, 1)

            def add_expert(b, qb, e):
                unit = 2 * b + qb
                dve.wait_ge(s_h1_used, NE * NC * unit + NC * (e + 1))
                for t in range(TU):
                    last = v.scalar_tensor_tensor(out=acc[:, t, :], in0=y_ps[:, t, :], scalar=w8[:, t, e:e + 1],
                                                  in1=acc[:, t, :], op0=ALU.mult, op1=ALU.add)
                last.then_inc(s_y_free, 1)
                dve.wait_ge(s_y_free, NE * unit + e + 1)

            def finish(item, b, qb):
                kind, unit = item[0], 2 * b + qb
                if kind == "turn":
                    k, p = item[1], full()
                    o = p.rearrange("p (t h r) -> p t h r", t=TU, h=REP)
                    link(v.reciprocal(den[:, :, :], o[:, :, :, HD]))
                    d = spread(den[:, :, :].rearrange("p t (h a) -> p t h a", a=1), 3, HD)
                    to = o_tok[:, :, k * REP * HD:(k + 1) * REP * HD].rearrange("p t (h d) -> p t h d", d=HD)
                    v.tensor_tensor(to, o[:, :, :, 0:HD], d, ALU.mult).then_inc(s_bank_free, 1)
                if kind == "oT":
                    v.tensor_copy(o_t[:, :], full()).then_inc(s_bank_free, 1)
                if kind == "wo":
                    p = full()
                    res = x2[:, qb, :, :]
                    dve.wait_ge(s_x2_free[qb], 16 * (b + 1))
                    ga = spread(mod_bc[:, ds(b, 1), 0:D], 1, TU)
                    v.tensor_tensor(res, p.rearrange("p (t d) -> p t d", t=TU), ga, ALU.mult).then_inc(s_bank_free, 1)
                    dve.wait_ge(s_bank_free, use["base"] + use["n"])
                    link(v.tensor_tensor(res, res, x_all[:, ds(b * TB + qb * TU, TU), :], ALU.add))
                    for t in range(TU):
                        last = v.bn_stats(stats2[:, t, :], res[:, t, :])
                    link(last, plain=True)
                    for t in range(TU):
                        last = v.bn_aggr(mean_var2[:, t, :], stats2[:, t, :])
                    link(last)
                    link(v.tensor_scalar(var_e[:, 0:TU], mean_var2[:, :, 1], LN_EPS, None, ALU.add))
                    rsqrt(rstd2[:, :], var_e[:, 0:TU], TU)
                    for t in range(TU):
                        last = v.tensor_scalar(xn2[:, t, :], res[:, t, :], mean_var2[:, t, 0:1], rstd2[:, t:t + 1],
                                               ALU.subtract, ALU.mult)
                    last.then_inc(s_xn2, 1)
                    dve.wait_ge(s_xn2, unit + 1)
                    first2 = [spread(mod_bc[:, ds(b, 1), i * D:i * D + 2], 1, TU) for i in (2, 1)]
                    link(v.tensor_tensor(pick[:, :, :], xn2[:, :, 0:2], first2[0], ALU.mult))
                    link(v.tensor_tensor(pick[:, :, :], pick[:, :, :], first2[1], ALU.add))
                    s, m, r, over, sg = (pick_f[:, i, :] for i in range(5))
                    link(v.tensor_tensor(s, pick[:, :, 0], pick[:, :, 1], ALU.add))
                    link(v.tensor_scalar(m, s, -1.0, None, ALU.mult))
                    link(v.tensor_tensor(m, m, s, ALU.max))
                    link(v.tensor_copy(pick_i[:, 0, :], m))
                    link(v.tensor_copy(r, pick_i[:, 0, :]))
                    link(v.tensor_tensor(over, r, m, ALU.is_gt))
                    link(v.tensor_tensor(r, r, over, ALU.subtract))
                    link(v.tensor_scalar(sg, s, 0.0, 2.0, ALU.is_ge, ALU.mult))
                    link(v.scalar_tensor_tensor(out=r, in0=sg, scalar=-1.0, in1=r, op0=ALU.add, op1=ALU.mult))
                    link(v.tensor_copy(pick_i[:, 0, :], r))
                    link(v.tensor_scalar(pick_i[:, 1, :], pick_i[:, 0, :], NE - 1, None, ALU.bitwise_and))
                    h = spread(pick_i[:, 1, :].rearrange("p (t a) -> p t a", a=1), 2, NE)
                    link(v.tensor_tensor(near[:, :, :], expert[:, :, :], h, ALU.subtract))
                    link(v.tensor_scalar(near[:, :, :], near[:, :, :], NE - 1, None, ALU.bitwise_and))
                    v.tensor_scalar(w8[:, :, :], near[:, :, :], 1.0, 0.5, ALU.is_le, ALU.mult).then_inc(s_w8, 1)
                    dve.wait_ge(s_w8, unit + 1)
                if kind == "ln2":
                    v.tensor_scalar(h2_t[:, :], full(), mod_t[:, 4, ds(b, 1)], mod_t[:, 3, ds(b, 1)],
                                    ALU.mult, ALU.add).then_inc(s_bank_free, 1)
                if kind == "w8":
                    v.tensor_copy(w8_t[:, :], full()[0:NE, :]).then_inc(s_bank_free, 1)
                if kind == "b2":
                    v.tensor_copy(acc[:, :, :], full().rearrange("p (t d) -> p t d", t=TU)).then_inc(s_bank_free, 1)
                    dve.wait_ge(s_bank_free, use["base"] + use["n"])
                if kind == "ffn":
                    u, p = item[1], full()
                    if u >= 2:
                        dve.wait_ge(s_h1_used, NE * NC * unit + u - 1)
                    v.tensor_scalar(h1[:, u % 2, :], p, b1_sb[:, u:u + 1], 0.0, ALU.add, ALU.max).then_inc(s_bank_free, 1)
                    if u and u % NC == 0:
                        add_expert(b, qb, u // NC - 1)
                if kind == "end":
                    add_expert(b, qb, NE - 1)
                    gb = spread(mod_bc[:, ds(b, 1), 3 * D:4 * D], 1, TU)
                    link(v.tensor_tensor(acc[:, :, :], acc[:, :, :], gb, ALU.mult))
                    v.tensor_tensor(x2[:, qb, :, :], x2[:, qb, :, :], acc[:, :, :], ALU.add).then_inc(s_out, 1)
                    dve.wait_ge(s_out, unit + 1)

            def phase(b, qb, where, items):
                begin(where, b - (where == "even") if where != "first" else 0)
                before = (b, 0) if qb else (b - 1, 1)
                nkb = KB_OF[qb]
                for l in range(SLOTS_OF[qb]):
                    if l == 0 and where != "first":
                        evacuate(*before, NKV - 1)
                    elif l and l % nkb == 0:
                        evacuate(b, qb, l // nkb - 1)
                    for item in items[l]:
                        if item in PREP:
                            prep(item, b + 1)
                        elif item[0] not in ("v0", "v1"):
                            finish(item, *before)

            dve.wait_ge(s_x0, 16)
            for item in PREP:
                prep(item, 0)
            phase(0, 0, "first", PLAN_FIRST)
            dve.wait_ge(s_x, 16)
            dve.wait_ge(s_ffn_in, 64)
            before_loop = chain["n"]
            with dve.Fori(0, NB - 1) as b:
                chain.update(base=before_loop + b * CHAIN_LOOP, n=0)
                phase(b, 1, "odd", PLAN_ODD)
                phase(b + 1, 0, "even", PLAN_EVEN)
                chain_counts["loop"] = chain["n"]
            chain.update(base=before_loop + (NB - 1) * CHAIN_LOOP, n=0)
            phase(NB - 1, 1, "last", PLAN_LAST)
            evacuate(NB - 1, 1, NKV - 1)
            begin("tail", NB - 1)
            for item in PLAN_TAIL[0]:
                finish(item, NB - 1, 1)


def rope_tables():
    inv = (np.float32(1.0) / np.float32(10000.0) ** (np.arange(0, HD, 2, dtype=np.float32) / np.float32(HD))).astype(np.float32)
    angle = np.outer(np.arange(SEQ, dtype=np.float32), inv).astype(np.float32)
    angle = np.concatenate([angle, angle], axis=-1)
    sign = np.where(np.arange(HD) < HD // 2, -1.0, 1.0).astype(np.float32)
    return np.stack([np.cos(angle), np.sin(angle) * sign]).astype(np.float32)


def kernel(**inputs):
    import concourse.bacc as bacc
    from concourse.bass_utils import run_bass_kernel_spmd

    nc = bacc.Bacc("TRN2", target_bir_lowering=False, num_devices=1)
    given = {n.removeprefix("L0_"): np.asarray(a) for n, a in inputs.items()}
    arrays = {
        "x": given["attn_x"],
        "wqkv": np.concatenate([given["attn_Wq"], given["attn_Wk"], given["attn_Wv"]]).T,
        "wo": given["attn_Wo"].T,
        "q_w": given["attn_q_norm_w"],
        "k_w": given["attn_k_norm_w"],
        "w1": given["ffn_W1"],
        "b1": given["ffn_b1"].reshape(NE * NC, P).T,
        "w2": given["ffn_W2"],
        "b2": given["ffn_b2"],
        "c": given["c"].T,
        "wmod": given["wmod"],
        "rope": rope_tables(),
    }
    arrays = {f"in_{n}": np.ascontiguousarray(a) for n, a in arrays.items()}
    args = [nc.dram_tensor(n, a.shape, mybir.dt.from_np(a.dtype), kind="ExternalInput").ap() for n, a in arrays.items()]
    args.append(nc.dram_tensor("out", (NB, SEQ, D), F32, kind="ExternalOutput").ap())
    counts = {}
    adaln_block(nc, *args, counts)
    assert counts["loop"] == CHAIN_LOOP, counts
    r = run_bass_kernel_spmd(nc, [arrays], core_ids=[0])
    return r.results[0]["out"]
```

```python
from contextlib import ExitStack

import numpy as np

import concourse.bass as bass
from concourse import mybir

ALU = mybir.AluOpType
ACT = mybir.ActivationFunctionType
F32 = mybir.dt.float32
BF16 = mybir.dt.bfloat16
I32 = mybir.dt.int32
AX = mybir.AxisListType

P = 128
NB, SEQ, D = 4, 1024, 128
NH, NKV, HD = 16, 4, 8
REP = NH // NKV
NQK = NH + NKV
NE, DFF = 8, 512
NC = DFF // P
QB = 512
TU = QB // P
TB = SEQ // P
NPIECE = 3
KR = NPIECE * NPIECE * HD
CAP = 30.0
SCALE = float(HD) ** -0.5
LN_EPS, RMS_EPS = 1e-5, 1e-6
QKVW = (NH + 2 * NKV) * HD
VW = 32
RING = 4

KB_OF = (TU, 2 * TU)
SLOTS_OF = (NKV * KB_OF[0], NKV * KB_OF[1])
SLOTS = sum(SLOTS_OF)
assert SLOTS % RING == 0 and SLOTS_OF[0] % RING == 0

SETUP_USES = 1 + NB
PREP = ["stat", "root", "xn", "lnT", "qkv0", "qkv1", "square", "rms", "rroot", "heads", "spin_q", "spin_k",
        "qT", "qT2", "kT", "kT2"]
WITH_BANK = {"lnT", "qkv0", "qkv1", "qT", "kT", "turn", "oT", "wo", "rank", "hsT", "ffn", "w8", "b2"}

STEPS = (2 * QB + NE * (P - 1)) // P
QUARTERS = -(-STEPS // TU)
WROW = 2 * DFF + NC
WRING = 4
LEAD = 2
NOW = 7


def prep_items(back):
    return [(what, 0, back) for what in PREP]


CHAIN = ["oT", "wo", "stat2", "root2", "xn2", "pick", "pick2", "rank", "place", "steps"]


def slot_shape(qb, l):
    kv, kb = divmod(l, KB_OF[qb])
    d = kb - TU * qb
    return kv, kb, max(d, 0) * P, d >= 0


def quarter_steps(q):
    return min(TU, STEPS - TU * q)


def experts(steps, following):
    out = []
    ahead = steps + following
    for j, (u, back) in enumerate(steps):
        items = []
        if u == 0 and j == 0:
            items.append(("hsT", 0, back))
        if u == STEPS - 1 and j + 1 < len(steps):
            items.append(("hsT", 0, steps[j + 1][1]))
        if (u + 1) % TU == 0 and u + 1 < STEPS:
            items.append(("hsT", (u + 1) // TU, back))
        items.append(("ffn", u, back))
        if j + LEAD < len(ahead):
            items.append(("weights", *ahead[j + LEAD]))
        if u == STEPS - 1:
            items.append(("end", 0, back))
        out.append(items)
    return out


EARLY = [(u, 2) for u in range(NOW, STEPS)]
LATE = [(u, 2) for u in range(STEPS)] + [(u, 1) for u in range(NOW)]
LATEST = [(u, back) for back in (2, 1) for u in range(STEPS)]
FIRST = [(u, 1) for u in range(NOW)]
TAIL = [(u, 1) for u in range(STEPS)]


def shift(steps):
    return [(u, back - 1) for u, back in steps[:LEAD]]


def plan(kind, qb):
    nkb, n = KB_OF[qb], SLOTS_OF[qb]
    at = [[] for _ in range(n)]

    def put(slot, *items):
        at[min(slot, n - 1)] += items

    def along(count, first, last):
        long = [QB - slot_shape(qb, l)[2] for l in range(first, last)]
        ends = np.cumsum(long)
        return [first + int(np.searchsorted(ends, (j + 0.5) * ends[-1] / count)) for j in range(count)]

    for k in range(NKV - 1):
        put((k + 1) * nkb + 1, ("turn", k, 0))
    if (kind, qb) == ("first", 0):
        for slot, item in zip(along(len(PREP), 0, 12), prep_items(-1)):
            put(slot, item)
        put(13, ("stacks", 0, -1), ("v", 0, -1))
        return at
    if qb == 0:
        put(0, ("stacks", 0, -1))
        put(8, ("v", 0, -1))
    elif kind != "last":
        for back, first, last in ((-1, 2, 15), (-2, 15, 30)):
            for slot, item in zip(along(len(PREP), first, last), prep_items(back)):
                put(slot, item)
        put(18, ("stacks", 0, -1))
        put(30, ("v", 0, -1))
    put(1, ("turn", NKV - 1, 1))
    for what, slot in zip(CHAIN, (2, 3, 3, 4, 4, 5, 5, 6, 7, 7) if qb else (2, 3, 4, 4, 5, 5, 6, 7, 7, 7)):
        put(slot, (what, 0, 1))
    for t in range(TU):
        put(8 + t, ("scatter", t, 1))
    put(12, ("sorted", 0, 1))
    if qb and kind != "first":
        for t in range(TU):
            put(t, ("gather", t, 3))
        put(2, ("w8", 0, 3))
        put(6, ("b2", 0, 3))
    following = shift(EARLY)
    if kind == "first":
        steps, first, last = FIRST, 18, n
        put(12, ("weights", 0, 1), ("weights", 1, 1))
    elif qb == 0:
        steps, first, last = EARLY, 0, n
        following = shift(LATE)
    elif kind == "mid":
        steps, first, last = LATE, 0, n
    else:
        steps, first, last = LATEST, 0, n
        following = []
    for slot, items in zip(along(len(steps), first, last), experts(steps, following)):
        put(slot, *items)
        if qb and items[-1][0] == "end" and items[-1][2] == 2:
            for t in range(TU):
                put(slot + 2 + t, ("gather", t, 2))
            put(slot + 8, ("w8", 0, 2), ("b2", 0, 2))
    return at


PLAN = {
    (kind, qb): plan(kind, qb) for kind in ("first", "mid", "last") for qb in range(2)
}


def tail():
    out = [("turn", NKV - 1, 1)]
    out += [("gather", t, 2) for t in range(TU)]
    out += [(what, 0, 1) for what in CHAIN]
    out += [("weights", u, 1) for u in range(LEAD)]
    out += [("scatter", t, 1) for t in range(TU)]
    out += [("sorted", 0, 1), ("w8", 0, 2), ("b2", 0, 2)]
    for items in experts(TAIL, []):
        out += items
    out += [("gather", t, 1) for t in range(TU)] + [("w8", 0, 1), ("b2", 0, 1)]
    return out


PLAN_TAIL = tail()
for phase_of in (("first", 1), ("mid", 1)):
    banked = [i for slot in PLAN[phase_of] for i in slot if i[0] in WITH_BANK]
    assert banked[-1] == ("ffn", NOW - 1, 1)


def uses(items):
    return sum(i[0] in WITH_BANK for i in items)


def uses_of(p):
    return sum(uses(s) for s in p)


USES_SETUP = SETUP_USES + uses(prep_items(0))
USES = {kind: uses_of(PLAN[kind, 0]) + uses_of(PLAN[kind, 1]) for kind in ("first", "mid", "last")}
assert USES["mid"] % 2 == 0


def use_base(kind, qb, i):
    if kind == "setup":
        return 0
    base = USES_SETUP + (uses_of(PLAN[kind, 0]) if qb == 1 else 0)
    if kind == "mid":
        base += USES["first"] + i * USES["mid"]
    if kind in ("last", "tail"):
        base += USES["first"] + (NB - 2) * USES["mid"] + (USES["last"] if kind == "tail" else 0)
    return base


def slot_base(b, qb):
    return b * SLOTS + qb * SLOTS_OF[0]


def diagonals(qb, l):
    return sum(slot_shape(qb, i)[3] for i in range(l))


def unit_of(b, qb, back):
    half = (qb - back) % 2
    return b - (back - qb + half) // 2, half, 2 * b + qb - back


def spread(ap, axis, n):
    shape = list(ap.shape)
    assert shape[axis] == 1
    shape[axis] = n
    return ap.broadcast_to(tuple(shape))


def wait(eng, sem, value):
    if isinstance(value, int) and value <= 0:
        return
    eng.wait_ge(sem, value)


CHAIN_LOOP = 178


def adaln_block(nc, x, wqkv, wo, q_w, k_w, weights, b2, c, wmod, rope, out, chain_counts):
    ctx = ExitStack()
    with ctx:
        def sb(name, shape, dt=F32):
            return ctx.enter_context(nc.sbuf_tensor(name, shape, dt))

        def ps(name, shape, dt=F32):
            return ctx.enter_context(nc.psum_tensor(name, shape, dt))

        def sem(name):
            return ctx.enter_context(nc.semaphore(name))

        x_all = sb("x_all", [P, NB * TB, D])
        w_ring = sb("w_ring", [P, WRING, WROW])
        b2_sb = sb("b2_sb", [NE, D])
        wqkv_t = sb("wqkv_t", [P, QKVW])
        wo_t = sb("wo_t", [P, D])
        c_t = sb("c_t", [P, NB])
        silu_w = sb("silu_w", [P, 3, NB])
        mod_t = sb("mod_t", [P, 6, NB])
        gates = sb("gates", [P, NB, 2, D])
        mod_pick = sb("mod_pick", [P, NB, 2, 2])
        ident = sb("ident", [P, P])
        expert = sb("expert", [P, TU, NE], I32)
        rope_sb = sb("rope_sb", [P, 2, TB, HD])
        qk_w = sb("qk_w", [P, 2, HD])
        rope_w = sb("rope_w", [P, 2, 2, TB, HD])
        Q = [sb(f"q_stack{i}", [KR, NH, QB], BF16) for i in range(2)]
        K = [sb(f"k_stack{i}", [KR, i + 1, NKV, QB], BF16) for i in range(2)]
        V = [sb(f"v_pad{i}", [P, KB_OF[i], NKV, VW]) for i in range(2)]
        probs = sb("probs", [P, RING, REP, QB])
        early = probs[:, RING - 1, :, :].rearrange("p h q -> p (h q)")
        wmod_sb = early[:, 3 * D:9 * D]
        silu_bc = probs[:, RING - 2, 0, :].rearrange("p (b c) -> p b c", b=NB)
        stats = sb("stats", [P, TU, 6])
        mean_var = sb("mean_var", [P, TU, 2])
        rstd = sb("rstd", [P, TU])
        nw_a = sb("nw_a", [P, TU * NQK])
        nw_i = sb("nw_i", [P, TU * NQK], I32)
        var_e = sb("var_e", [P, TU])
        mean_sq = sb("mean_sq", [P, TU * NQK])
        rms = sb("rms", [P, TU * NQK])
        xn = sb("xn", [P, TU, D])
        h_t = sb("h_t", [P, QB])
        qkv = sb("qkv", [P, TB, QKVW])
        rot_a = sb("rot_a", [P, TU, NQK * HD])
        rot_b = sb("rot_b", [P, TU, NQK * HD])
        k_rot = sb("k_rot", [P, TU, NKV * HD])
        rest = sb("rest", [P, QB])
        q_pieces = sb("q_pieces", [P, NPIECE, QB], BF16)
        k_pieces = sb("k_pieces", [NKV * HD, NPIECE, QB], BF16)
        o_sb = sb("o_sb", [P, 2, QB])
        den = sb("den", [P, TU, REP])
        o_tok = sb("o_tok", [P, TU, D])
        o_t = sb("o_t", [P, QB])
        attn = sb("attn", [P, TU, D])
        xn2 = sb("xn2", [P, TU, D])
        stats2 = sb("stats2", [P, TU, 6])
        mean_var2 = sb("mean_var2", [P, TU, 2])
        rstd2 = sb("rstd2", [P, TU])
        pick = sb("pick", [P, TU, 2])
        pick_f = sb("pick_f", [P, 5, TU])
        pick_i = sb("pick_i", [P, 2, TU], I32)
        near = sb("near", [P, TU, NE], I32)
        w8 = sb("w8", [P, 2, TU, NE])
        w8_t = sb("w8_t", [NE, QB])
        before2 = sb("before2", [P, P])
        all2 = sb("all2", [P, P])
        up_to = sb("up_to", [P, NE, NE])
        step_i = sb("step_i", [P, QUARTERS * TU, NE], I32)
        step_no = sb("step_no", [P, QUARTERS * TU, NE])
        row_i = sb("row_i", [P, 1], I32)
        row_no = sb("row_no", [P, 1])
        rank = sb("rank", [P, 2, TU, NE])
        n_steps_i = sb("n_steps_i", [P, NE], I32)
        n_steps = sb("n_steps", [P, NE])
        up_to_n = sb("up_to_n", [P, NE, NE])
        ends = sb("ends", [P, NE])
        starts = sb("starts", [P, NE])
        place_of = sb("place_of", [P, 2, TU, NE])
        place_f = sb("place_f", [P, 2, TU])
        place = sb("place", [P, 2, 2, TU], I32)
        over_end = sb("over_end", [P, QUARTERS * TU, NE])
        of_step = sb("of_step", [P, QUARTERS * TU])
        w_row = sb("w_row", [P, 2, QUARTERS * TU], I32)
        h_sorted = sb("h_sorted", [P, STEPS, D])
        h2_t = sb("h2_t", [P, 2, QB])
        h1 = sb("h1", [P, 2, NC, P])
        y_sb = sb("y_sb", [P, 2, TU, D])
        y_tok = sb("y_tok", [P, 2, TU, D])

        scores = ps("scores", [P, REP, QB])
        o_ps = ps("o_ps", [P, QB])
        bank = ps("bank", [P, 2, QB])
        y_ps = ps("y_ps", [P, TU, D])

        q_dram = nc.dram_tensor("q_dram", (NB, 2, NPIECE, HD, NH, QB), BF16, kind="Internal").ap()
        k_dram = nc.dram_tensor("k_dram", (NB, 2, NPIECE, HD, NKV, QB), BF16, kind="Internal").ap()

        h_dram = [nc.dram_tensor(f"h_dram{i}", (STEPS * P, D), F32, kind="Internal").ap() for i in range(2)]
        y_dram = [nc.dram_tensor(f"y_dram{i}", (STEPS * P, D), F32, kind="Internal").ap() for i in range(2)]

        s_alone = sem("s_alone")
        s_small = sem("s_small")
        s_x0 = sem("s_x0")
        s_x = sem("s_x")
        s_rope_in = sem("s_rope_in")
        s_b2 = sem("s_b2")
        s_const = sem("s_const")
        s_tables = sem("s_tables")
        s_exp0 = sem("s_exp0")
        s_silu = sem("s_silu")
        s_xn = sem("s_xn")
        s_chain = sem("s_chain")
        s_bank_full = sem("s_bank_full")
        s_bank_free = sem("s_bank_free")
        s_roped = sem("s_roped")
        s_split = sem("s_split")
        s_stored = sem("s_stored")
        s_stack = [sem("s_stack0"), sem("s_stack1")]
        s_v = [sem("s_v0"), sem("s_v1")]
        s_scored = sem("s_scored")
        s_tanh = sem("s_tanh")
        s_exp = sem("s_exp")
        s_masked = sem("s_masked")
        s_pv = sem("s_pv")
        s_o = sem("s_o")
        s_xn2 = sem("s_xn2")
        s_w8 = sem("s_w8")
        s_place = sem("s_place")
        s_w_row = sem("s_w_row")
        s_zero = sem("s_zero")
        s_h_zero = sem("s_h_zero")
        s_scattered = sem("s_scattered")
        s_sorted = sem("s_sorted")
        s_turned = sem("s_turned")
        s_weights = [sem(f"s_weights{i}") for i in range(WRING)]
        s_h1_used = sem("s_h1_used")
        s_y_free = sem("s_y_free")
        s_y_stored = [sem(f"s_y_stored{i}") for i in range(2)]
        s_gathered = sem("s_gathered")
        s_sum = sem("s_sum")
        s_out = sem("s_out")

        def ds(i, n):
            return slice(i, i + n) if isinstance(i, int) else bass.ds(i, n)

        STORES = 2 * NPIECE
        LOADS = (NPIECE + 1, NPIECE + 2)

        CONSTS = 14

        block = ctx.enter_context(nc.Block())

        @block.sync
        def _(sp):
            sp.dma_start(c_t[:, :], c).then_inc(s_small, 16)
            sp.dma_start(wmod_sb[:, :], wmod).then_inc(s_small, 16)
            sp.dma_start(wqkv_t[:, :], wqkv).then_inc(s_small, 16)
            sp.dma_start(wo_t[:, :], wo).then_inc(s_small, 16)
            xt = x.rearrange("b (t p) d -> p (b t) d", p=P)
            sp.dma_start(x_all[:, 0:TU, :], xt[:, 0:TU, :]).then_inc(s_x0, 16)
            sp.dma_start(rope_sb[:, :, :, :], rope.rearrange("f (t p) d -> p f t d", p=P)).then_inc(s_rope_in, 16)
            sp.dma_start(qk_w[:, 0, :], spread(q_w.rearrange("(a d) -> a d", a=1), 0, P)).then_inc(s_rope_in, 16)
            sp.dma_start(qk_w[:, 1, :], spread(k_w.rearrange("(a d) -> a d", a=1), 0, P)).then_inc(s_rope_in, 16)
            sp.dma_start(x_all[:, TU:, :], xt[:, TU:, :]).then_inc(s_x, 16)
            sp.dma_start(b2_sb[:, :], b2).then_inc(s_b2, 16)
            sp.wait_ge(s_zero, 1)
            for i in range(2):
                sp.dma_start(h_dram[i].rearrange("(s p) d -> p s d", p=P), spread(y_sb[:, 0, 0:1, :], 1, STEPS)) \
                    .then_inc(s_h_zero, 16)

            def store_pieces(b, half):
                sp.wait_ge(s_split, 2 * (2 * b + half) + 2)
                sp.sem_inc(s_alone, 1)
                for i in range(NPIECE):
                    for dst, src in ((k_dram, k_pieces), (q_dram, q_pieces)):
                        dst = dst[ds(b, 1), half, i, :, :, :].rearrange("a d h t -> h (a d) t")
                        sp.dma_start(dst, src[:, i, :]).then_inc(s_stored, 16)

            def load_stacks(b, qb):
                sp.wait_ge(s_stored, 16 * STORES * (2 * b + qb + 1))
                sp.sem_inc(s_alone, 1)
                wait(sp, s_scored, 2 * (slot_base(b, 0) if qb else slot_base(b, 0) - SLOTS_OF[1]))
                sp.sem_inc(s_alone, 1)
                for half in range(qb + 1):
                    src = k_dram[ds(b, 1), half, :, :, :, :].rearrange("a j d h t -> a (j d) (h t)")
                    sp.dma_start(K[qb][:, half, :, :], spread(src, 0, NPIECE)).then_inc(s_stack[qb], 16)
                for i in range(NPIECE):
                    src = q_dram[ds(b, 1), qb, i, :, :, :].rearrange("a d h t -> a d (h t)")
                    rows = slice(i * NPIECE * HD, (i + 1) * NPIECE * HD)
                    sp.dma_start(Q[qb][rows, :, :], spread(src, 0, NPIECE)).then_inc(s_stack[qb], 16)

            xo = out.rearrange("b (t p) d -> p (b t) d", p=P)

            def store_out(b, qb):
                sp.wait_ge(s_sum, 2 * b + qb + 2)
                sp.sem_inc(s_alone, 1)
                here = ds(b * TB + qb * TU, TU)
                sp.dma_start(xo[:, here, :], x_all[:, here, :]).then_inc(s_out, 16)

            def load_sorted(qb, unit):
                sp.wait_ge(s_scattered, 16 * 2 * TU * (unit + 1))
                sp.sem_inc(s_alone, 1)
                wait(sp, s_turned, QUARTERS * unit)
                sp.sem_inc(s_alone, 1)
                sp.dma_start(h_sorted[:, :, :], h_dram[qb].rearrange("(s p) d -> p s d", p=P)).then_inc(s_sorted, 16)

            def store_y(qb, unit, q):
                sp.wait_ge(s_y_free, QUARTERS * unit + q + 1)
                sp.sem_inc(s_alone, 1)
                if q == 0:
                    wait(sp, s_sum, unit)
                    sp.sem_inc(s_alone, 1)
                n = quarter_steps(q)
                rows = y_dram[qb][q * TU * P:(q * TU + n) * P, :]
                sp.dma_start(rows.rearrange("(s p) d -> p s d", p=P), y_sb[:, q % 2, 0:n, :]).then_inc(s_y_stored[q % 2], 16)

            def do(item, b, qb):
                kind, which, back = item
                ub, uqb, unit = unit_of(b, qb, back)
                if kind == "kT2":
                    store_pieces(ub, uqb)
                if kind == "stacks":
                    load_stacks(ub, uqb)
                if kind == "sorted":
                    load_sorted(uqb, unit)
                if kind == "ffn" and which and which % TU == 0:
                    store_y(uqb, unit, which // TU - 1)
                if kind == "end":
                    store_y(uqb, unit, QUARTERS - 1)
                if kind == "b2":
                    store_out(ub, uqb)

            def phase(b, qb, kind):
                for slot in PLAN[kind, qb]:
                    for item in slot:
                        do(item, b, qb)

            store_pieces(0, 0)
            load_stacks(0, 0)
            for qb in range(2):
                phase(0, qb, "first")
            with sp.Fori(0, NB - 2) as i:
                for qb in range(2):
                    phase(i + 1, qb, "mid")
            for qb in range(2):
                phase(NB - 1, qb, "last")
            for item in PLAN_TAIL:
                do(item, NB, 0)
            sp.wait_ge(s_out, 16 * 2 * NB)

        @block.gpsimd
        def _(pool):
            own = [0]

            def done(ins):
                own[0] += 1
                ins.then_inc(s_const, 1)

            done(nc.gpsimd.memset(ident[:, :], 0.0))
            done(nc.gpsimd.iota(expert[:, :, :], pattern=[[0, TU], [1, NE]], base=0, channel_multiplier=0))
            done(nc.gpsimd.iota(step_i[:, :, :], pattern=[[1, QUARTERS * TU], [0, NE]], base=0, channel_multiplier=0))
            done(nc.gpsimd.iota(row_i[:, :], pattern=[[0, 1]], base=0, channel_multiplier=1))
            done(nc.gpsimd.memset(before2[:, :], 2.0))
            done(nc.gpsimd.memset(all2[:, :], 2.0))
            done(nc.gpsimd.memset(up_to[:, :, :], 1.0))
            nc.gpsimd.memset(y_sb[:, 0, 0, :], 0.0).then_inc(s_zero, 1)
            for v in V:
                done(nc.gpsimd.memset(v[:, :, :, :], 0.0))
            pool.wait_ge(s_const, own[0])
            done(nc.gpsimd.affine_select(out=ident[:, :], in_=ident[:, :], compare_op=ALU.not_equal, fill=1.0, base=0,
                                         pattern=[[-1, P]], channel_multiplier=1))
            done(nc.gpsimd.affine_select(out=before2[:, :], in_=before2[:, :], compare_op=ALU.is_ge, fill=0.0, base=-1,
                                         pattern=[[1, P]], channel_multiplier=-1))
            done(nc.gpsimd.affine_select(out=up_to[:, :, :], in_=up_to[:, :, :], compare_op=ALU.is_ge, fill=0.0, base=0,
                                         pattern=[[1, NE], [-1, NE]], channel_multiplier=0))
            for v in V:
                done(nc.gpsimd.memset(v[:, :, :, HD:HD + 1], 1.0))
            pool.wait_ge(s_const, own[0])
            pool.wait_ge(s_rope_in, 48)
            for n in range(2):
                w = spread(qk_w[:, n:n + 1, :], 1, TB)
                nc.gpsimd.tensor_tensor(rope_w[:, 0, n, :, :], rope_sb[:, 0, :, :], w, ALU.mult).then_inc(s_tables, 1)
                for half in range(2):
                    here = slice(half * HD // 2, (half + 1) * HD // 2)
                    there = slice((1 - half) * HD // 2, (2 - half) * HD // 2)
                    nc.gpsimd.tensor_tensor(rope_w[:, 1, n, :, here], rope_sb[:, 1, :, here],
                                            w[:, :, there], ALU.mult).then_inc(s_tables, 1)
            def pad_values(b, qb):
                pool.wait_ge(s_roped, 2 * b + qb + 1)
                wait(pool, s_pv, slot_base(b, 0) if qb else slot_base(b, 0) - SLOTS_OF[1])
                pool.sem_inc(s_alone, 1)
                src = qkv[:, 0:KB_OF[qb], NQK * HD:].rearrange("p t (k d) -> p t k d", d=HD)
                nc.gpsimd.tensor_copy(V[qb][:, :, :, 0:HD], src).then_inc(s_v[qb], 1)

            def pool_wait(sem, value):
                wait(pool, sem, value)
                pool.sem_inc(s_alone, 1)

            def scatter(qb, unit, t):
                if t == 0:
                    pool_wait(s_xn2, unit + 1)
                    pool_wait(s_place, unit + 1)
                    pool_wait(s_sorted, 16 * unit)
                for j in range(2):
                    to = bass.IndirectOffsetOnAxis(place[:, qb, j, t:t + 1], 0)
                    nc.gpsimd.indirect_dma_start(h_dram[qb], to, xn2[:, t, :], None).then_inc(s_scattered, 16)

            def load_weights(qb, unit, u):
                pool_wait(s_w_row, unit + 1)
                had = u - WRING if u >= WRING else max(range(u, STEPS, WRING)) - STEPS
                pool_wait(s_h1_used, STEPS * unit + had + 1)
                row = bass.IndirectOffsetOnAxis(w_row[:, qb, u:u + 1], 0)
                nc.gpsimd.indirect_dma_start(w_ring[:, u % WRING, :], None, weights, row).then_inc(s_weights[u % WRING], 16)

            def gather(qb, unit, t):
                if t == 0:
                    for i in range(2):
                        pool_wait(s_y_stored[i], 16 * (QUARTERS // 2 * (unit + 1) + 1))
                    pool_wait(s_sum, unit + 1)
                for j in range(2):
                    at = bass.IndirectOffsetOnAxis(place[:, qb, j, t:t + 1], 0)
                    nc.gpsimd.indirect_dma_start(y_tok[:, j, t, :], None, y_dram[qb], at).then_inc(s_gathered, 16)

            def do(item, b, qb):
                kind, which, back = item
                ub, uqb, unit = unit_of(b, qb, back)
                if kind == "v":
                    pad_values(ub, uqb)
                if kind == "scatter":
                    scatter(uqb, unit, which)
                if kind == "weights":
                    load_weights(uqb, unit, which)
                if kind == "gather":
                    gather(uqb, unit, which)

            def phase(b, qb, items):
                for l in range(SLOTS_OF[qb]):
                    g = slot_base(b, qb) + l
                    kv, kb, off, diagonal = slot_shape(qb, l)
                    if diagonal:
                        pool.wait_ge(s_exp, g + 1)
                        pool.sem_inc(s_alone, 1)
                        tri = probs[:, l % RING, :, off:off + P]
                        nc.gpsimd.affine_select(out=tri, in_=tri, compare_op=ALU.is_ge, fill=0.0, base=0,
                                                pattern=[[0, REP], [1, P]], channel_multiplier=-1).then_inc(s_masked, 1)
                    for item in items[l]:
                        do(item, b, qb)

            pool.sem_inc(s_sorted, 16)
            pool.sem_inc(s_sum, 1)
            for i in range(2):
                pool.sem_inc(s_y_stored[i], 16)
            pad_values(0, 0)
            phase(0, 0, PLAN["first", 0])
            pool.wait_ge(s_h_zero, 32)
            phase(0, 1, PLAN["first", 1])
            with pool.Fori(0, NB - 2) as i:
                for qb in range(2):
                    phase(i + 1, qb, PLAN["mid", qb])
            for qb in range(2):
                phase(NB - 1, qb, PLAN["last", qb])
            for item in PLAN_TAIL:
                do(item, NB, 0)

        @block.scalar
        def _(act):
            act.wait_ge(s_small, 16 * 4)
            nc.scalar.activation(silu_w[:, 0, :], c_t[:, :], ACT.Exp, scale=-1.0).then_inc(s_exp0, 1)

            def cap(b, qb, l):
                g = slot_base(b, qb) + l
                _, _, off, _ = slot_shape(qb, l)
                r = l % RING
                wait(act, s_pv, g - RING + 1)
                if off < QB // 2:
                    for pair in range(2):
                        act.wait_ge(s_scored, 2 * g + pair + 1)
                        h = slice(2 * pair, 2 * pair + 2)
                        nc.scalar.activation(probs[:, r, h, off:QB], scores[:, h, off:QB], ACT.Tanh,
                                             scale=SCALE / CAP).then_inc(s_tanh, 1)
                else:
                    act.wait_ge(s_scored, 2 * g + 2)
                    nc.scalar.activation(probs[:, r, :, off:QB], scores[:, :, off:QB], ACT.Tanh,
                                         scale=SCALE / CAP).then_inc(s_tanh, 2)

            def exponential(b, qb, l):
                g = slot_base(b, qb) + l
                _, _, off, _ = slot_shape(qb, l)
                p = probs[:, l % RING, :, off:QB]
                act.wait_ge(s_tanh, 2 * g + 2)
                nc.scalar.activation(p, p, ACT.Exp, scale=CAP).then_inc(s_exp, 1)

            def phase(b, qb, last=False):
                n = SLOTS_OF[qb]
                for l in range(n):
                    if l + 1 < n:
                        cap(b, qb, l + 1)
                    elif not last:
                        cap(b + qb, 1 - qb, 0)
                    exponential(b, qb, l)

            cap(0, 0, 0)
            phase(0, 0)
            phase(0, 1)
            with act.Fori(0, NB - 2) as i:
                phase(i + 1, 0)
                phase(i + 1, 1)
            phase(NB - 1, 0)
            phase(NB - 1, 1, last=True)

        @block.tensor
        def _(pe):
            use = {}

            def begin(kind, qb=0, i=0):
                use.update(base=use_base(kind, qb, i), n=0, parity=use_base(kind, qb, 0) % 2)

            def take():
                n = use["base"] + use["n"]
                wait(pe, s_bank_free, n - 1)
                p = bank[:, (use["parity"] + use["n"]) % 2, :]
                use["n"] += 1
                return p, n

            def read_of(n):
                pe.wait_ge(s_bank_free, n + 1)

            def transposes(p, src_of, rows=P):
                for t in range(TU):
                    last = nc.tensor.transpose(p[0:rows, t * P:(t + 1) * P], src_of(t), ident[:, :])
                last.then_inc(s_bank_full, 1)

            begin("setup")
            pe.wait_ge(s_small, 16 * 4)
            pe.wait_ge(s_const, CONSTS)
            pe.wait_ge(s_silu, 1)
            p, _ = take()
            for i in range(6):
                last = nc.tensor.matmul(p[:, i * NB:(i + 1) * NB], wmod_sb[:, i * D:(i + 1) * D], silu_w[:, 2, :],
                                        start=True, stop=True)
            last.then_inc(s_bank_full, 1)
            def prep(item, own_b, own_qb, marks):
                kind = item[0]
                b, half, _ = unit_of(own_b, own_qb, item[2])
                if kind == "lnT":
                    pe.wait_ge(s_xn, 2 * b + half + 1)
                    p, n = take()
                    transposes(p, lambda t: xn[:, t, :])
                    marks[kind] = n
                if kind in ("qkv0", "qkv1"):
                    if kind == "qkv0":
                        read_of(marks["lnT"])
                    p, n = take()
                    for t in range(2):
                        i = 2 * (kind == "qkv1") + t
                        last = nc.tensor.matmul(p[:, t * QKVW:(t + 1) * QKVW], h_t[:, i * P:(i + 1) * P], wqkv_t[:, :],
                                                start=True, stop=True)
                    last.then_inc(s_bank_full, 1)
                if kind in ("qT", "kT"):
                    pe.wait_ge(s_roped, 2 * b + half + 1)
                    p, n = take()
                    if kind == "qT":
                        transposes(p, lambda t: rot_b[:, t, 0:NH * HD])
                    else:
                        transposes(p, lambda t: k_rot[:, t, :], rows=NKV * HD)

            def qk(b, qb, l):
                g = slot_base(b, qb) + l
                kv, kb, off, _ = slot_shape(qb, l)
                if l == 0:
                    pe.wait_ge(s_stack[qb], 16 * LOADS[qb] * (b + 1))
                for hh in range(REP):
                    if hh % 2 == 0:
                        wait(pe, s_tanh, 2 * (g - 1) + hh // 2 + 1)
                    last = nc.tensor.matmul(scores[:, hh, off:QB], K[qb][:, kb // TU, kv, kb % TU * P:(kb % TU + 1) * P],
                                            Q[qb][:, kv * REP + hh, off:QB], start=True, stop=True)
                    if hh % 2:
                        last.then_inc(s_scored, 1)

            def pv(b, qb, l):
                g = slot_base(b, qb) + l
                kv, kb, off, diagonal = slot_shape(qb, l)
                if l == 0:
                    pe.wait_ge(s_v[qb], b + 1)
                if kb == 0:
                    wait(pe, s_o, b * 2 * NKV + qb * NKV + kv)
                if diagonal:
                    pe.wait_ge(s_masked, b * 2 * NKV * TU + diagonals(0, qb * SLOTS_OF[0]) + diagonals(qb, l) + 1)
                else:
                    pe.wait_ge(s_exp, g + 1)
                for hh in range(REP):
                    last = nc.tensor.matmul(o_ps[32 * hh:32 * hh + VW, off:QB], V[qb][:, kb, kv, :],
                                            probs[:, l % RING, hh, off:QB], start=(kb == 0),
                                            stop=(kb == KB_OF[qb] - 1))
                last.then_inc(s_pv, 1)

            def finish(item, own_b, own_qb, marks):
                kind, which, back = item
                b, qb, unit = unit_of(own_b, own_qb, back)
                if kind == "turn":
                    k = which
                    pe.wait_ge(s_o, unit * NKV + k + 1)
                    p, n = take()
                    transposes(p, lambda t: o_sb[:, k % 2, t * P:(t + 1) * P])
                    marks[kind] = n
                if kind == "oT":
                    read_of(marks["turn"])
                    p, n = take()
                    transposes(p, lambda t: o_tok[:, t, :])
                    marks[kind] = n
                if kind == "wo":
                    read_of(marks["oT"])
                    p, n = take()
                    for t in range(TU):
                        last = nc.tensor.matmul(p[:, t * D:(t + 1) * D], o_t[:, t * P:(t + 1) * P], wo_t[:, :],
                                                start=True, stop=True)
                    last.then_inc(s_bank_full, 1)
                if kind == "rank":
                    pe.wait_ge(s_w8, unit + 1)
                    p, n = take()
                    tokens = w8[:, qb, :, :].rearrange("p t e -> p (t e)")
                    nc.tensor.matmul(p[:, 0:TU * NE], before2[:, :], tokens, start=True, stop=True)
                    nc.tensor.matmul(p[:, TU * NE:2 * TU * NE], all2[:, :], tokens, start=True, stop=True) \
                        .then_inc(s_bank_full, 1)
                if kind == "hsT":
                    if which == 0:
                        pe.wait_ge(s_sorted, 16 * (unit + 2))
                    p, n = take()
                    for t in range(quarter_steps(which)):
                        last = nc.tensor.transpose(p[:, t * P:(t + 1) * P], h_sorted[:, which * TU + t, :], ident[:, :])
                    last.then_inc(s_bank_full, 1)
                    marks[kind, which] = n
                if kind == "w8":
                    p, n = take()
                    transposes(p, lambda t: w8[:, qb, t, :], rows=NE)
                    marks[kind] = n
                if kind == "b2":
                    read_of(marks["w8"])
                    p, n = take()
                    for t in range(TU):
                        last = nc.tensor.matmul(p[:, t * D:(t + 1) * D], w8_t[:, t * P:(t + 1) * P], b2_sb[:, :],
                                                start=True, stop=True)
                    last.then_inc(s_bank_full, 1)
                if kind == "ffn":
                    u, q = which, which // TU
                    if u % TU == 0:
                        read_of(marks["hsT", q])
                    pe.wait_ge(s_weights[u % WRING], 16 * (len(range(u % WRING, STEPS, WRING)) * unit + u // WRING + 1))
                    p, n = take()
                    for ch in range(NC):
                        last = nc.tensor.matmul(p[:, ch * P:(ch + 1) * P], w_ring[:, u % WRING, ch * P:(ch + 1) * P],
                                                h2_t[:, q % 2, u % TU * P:(u % TU + 1) * P], start=True, stop=True)
                    last.then_inc(s_bank_full, 1)
                    if u:
                        second(u - 1, unit, marks["ffn"])
                    marks["ffn"] = n
                if kind == "end":
                    second(STEPS - 1, unit, marks["ffn"])

            def second(u, unit, n):
                read_of(n)
                if u % TU == 0:
                    wait(pe, s_y_free, QUARTERS * unit + u // TU)
                for ch in range(NC):
                    last = nc.tensor.matmul(y_ps[:, u % TU, :], h1[:, u % 2, ch, :],
                                            w_ring[:, u % WRING, DFF + ch * D:DFF + (ch + 1) * D],
                                            start=(ch == 0), stop=(ch == NC - 1))
                last.then_inc(s_h1_used, 1)

            def phase(b, qb, kind, i=0):
                begin(kind, qb, i)
                n, marks = SLOTS_OF[qb], dict(ffn=use["base"] - 1)
                items = PLAN[kind, qb]
                before = (b, 0) if qb else (b - 1, 1)
                for l in range(n):
                    if l + 1 < n:
                        qk(b, qb, l + 1)
                    elif (kind, qb) != ("last", 1):
                        qk(b + qb, 1 - qb, 0)
                    for item in items[l]:
                        if item[0] in PREP:
                            prep(item, b, qb, marks)
                        else:
                            finish(item, b, qb, marks)
                    if l:
                        pv(b, qb, l - 1)
                    elif (kind, qb) != ("first", 0):
                        pv(*before, SLOTS_OF[before[1]] - 1)

            marks = {}
            for item in prep_items(0):
                if item[0] in WITH_BANK:
                    prep(item, 0, 0, marks)
            pe.wait_ge(s_silu, 2)
            for b in range(NB):
                p, _ = take()
                nc.tensor.matmul(p[:, :], silu_bc[:, b, :], wmod_sb[:, 2 * D:], start=True, stop=True).then_inc(s_bank_full, 1)
            assert use["n"] == USES_SETUP
            qk(0, 0, 0)
            phase(0, 0, "first")
            pe.wait_ge(s_b2, 16)
            phase(0, 1, "first")
            with pe.Fori(0, NB - 2) as i:
                for qb in range(2):
                    phase(i + 1, qb, "mid", i)
            for qb in range(2):
                phase(NB - 1, qb, "last")
            pv(NB - 1, 1, SLOTS_OF[1] - 1)
            begin("tail")
            marks = dict(ffn=use["base"] - 1)
            for item in PLAN_TAIL:
                finish(item, NB, 0, marks)

        @block.vector
        def _(dve):
            v = nc.vector
            use, chain = {}, dict(base=0, n=0)

            def link(ins, plain=False):
                chain["n"] += 1
                ins.then_inc(s_chain, 1)
                dve.wait_ge(s_chain, chain["base"] + chain["n"])
                if plain:
                    dve.sem_inc(s_alone, 1)

            def begin(kind, qb=0, i=0):
                use.update(base=use_base(kind, qb, i), n=0, parity=use_base(kind, qb, 0) % 2)

            def full():
                dve.wait_ge(s_bank_full, use["base"] + use["n"] + 1)
                p = bank[:, (use["parity"] + use["n"]) % 2, :]
                use["n"] += 1
                return p

            def rsqrt(y, val, n):
                a, i = nw_a[:, 0:n], nw_i[:, 0:n]
                link(v.tensor_scalar(i, val.bitcast(I32), 1, None, ALU.logical_shift_right))
                link(v.tensor_scalar(y.bitcast(I32), i, -1.0, float(0x5F3759DF), ALU.mult, ALU.add))
                for _ in range(3):
                    link(v.scalar_tensor_tensor(out=a, in0=y, scalar=-0.5, in1=y, op0=ALU.mult, op1=ALU.mult))
                    link(v.tensor_tensor(a, a, val, ALU.mult))
                    link(v.scalar_tensor_tensor(out=y, in0=a, scalar=1.5, in1=y, op0=ALU.add, op1=ALU.mult))

            begin("setup")
            dve.wait_ge(s_exp0, 1)
            link(v.tensor_scalar(silu_w[:, 1, :], silu_w[:, 0, :], 1.0, None, ALU.add))
            link(v.reciprocal(silu_w[:, 1, :], silu_w[:, 1, :]))
            v.tensor_tensor(silu_w[:, 2, :], c_t[:, :], silu_w[:, 1, :], ALU.mult).then_inc(s_silu, 1)
            dve.wait_ge(s_silu, 1)
            v.tensor_copy(silu_bc[:, :, :], spread(silu_w[:, 2, :].rearrange("p (b a) -> p b a", a=1), 2, P)).then_inc(s_silu, 1)
            p = full()
            link(v.tensor_copy(mod_t[:, :, :], p[:, 0:6 * NB].rearrange("p (i b) -> p i b", b=NB)))
            for i in (1, 4):
                link(v.tensor_scalar(mod_t[:, i, :], mod_t[:, i, :], 1.0, None, ALU.add))
            v.tensor_copy(nw_a[:, 0:1], mod_t[:, 0, 0:1]).then_inc(s_bank_free, 1)
            def prep(item, own_b, own_qb):
                kind = item[0]
                b, half, _ = unit_of(own_b, own_qb, item[2])
                here = slice(half * TU, (half + 1) * TU)
                part = qkv[:, here, 0:NQK * HD]
                q_cols, k_cols, hh = slice(0, NH * HD), slice(NH * HD, NQK * HD), HD // 2

                def heads(ap):
                    return ap.rearrange("p t (h d) -> p t h d", d=HD)

                def table(f, n, count, cols=slice(0, HD)):
                    return spread(rope_w[:, f, n, here, cols].rearrange("p t (a d) -> p t a d", a=1), 2, count)

                def turned(src, n, count):
                    a, r = heads(rot_a[:, :, src]), heads(rot_b[:, :, src])
                    v.tensor_tensor(r[:, :, :, 0:hh], a[:, :, :, hh:], table(1, n, count, slice(0, hh)), ALU.mult)
                    link(v.tensor_tensor(r[:, :, :, hh:], a[:, :, :, 0:hh], table(1, n, count, slice(hh, HD)), ALU.mult))
                    link(v.tensor_tensor(a, a, table(0, n, count), ALU.mult))

                if kind == "stat":
                    for t in range(TU):
                        last = v.bn_stats(stats[:, t, :], x_all[:, ds(b * TB + half * TU + t, 1), :])
                    link(last, plain=True)
                    for t in range(TU):
                        last = v.bn_aggr(mean_var[:, t, :], stats[:, t, :])
                    link(last)
                if kind == "root":
                    link(v.tensor_scalar(var_e[:, :], mean_var[:, :, 1], LN_EPS, None, ALU.add))
                    rsqrt(rstd[:, :], var_e[:, :], TU)
                if kind == "xn":
                    for t in range(TU):
                        last = v.tensor_scalar(xn[:, t, :], x_all[:, ds(b * TB + half * TU + t, 1), :],
                                               mean_var[:, t, 0:1], rstd[:, t:t + 1], ALU.subtract, ALU.mult)
                    last.then_inc(s_xn, 1)
                if kind == "lnT":
                    v.tensor_scalar(h_t[:, :], full(), mod_t[:, 1, ds(b, 1)], mod_t[:, 0, ds(b, 1)],
                                    ALU.mult, ALU.add).then_inc(s_bank_free, 1)
                if kind in ("qkv0", "qkv1"):
                    p, t0 = full(), half * TU + 2 * (kind == "qkv1")
                    if kind == "qkv0":
                        wait(dve, s_v[1], b)
                    v.tensor_copy(qkv[:, t0:t0 + 2, :], p[:, 0:2 * QKVW].rearrange("p (t n) -> p t n", t=2)) \
                        .then_inc(s_bank_free, 1)
                    dve.wait_ge(s_bank_free, use["base"] + use["n"])
                if kind == "square":
                    link(v.tensor_tensor(rot_a[:, :, :], part, part, ALU.mult))
                if kind == "rms":
                    link(v.tensor_reduce(mean_sq[:, :], rot_a[:, :, :].rearrange("p t (h d) -> p (t h) d", d=HD),
                                         AX.X, ALU.add))
                    link(v.tensor_scalar(mean_sq[:, :], mean_sq[:, :], 1.0 / HD, RMS_EPS, ALU.mult, ALU.add))
                if kind == "rroot":
                    rsqrt(rms[:, :], mean_sq[:, :], TU * NQK)
                if kind == "heads":
                    if isinstance(b, int) and b == 0 and half == 0:
                        dve.wait_ge(s_tables, 6)
                    r = spread(rms[:, :].rearrange("p (t h a) -> p t h a", t=TU, a=1), 3, HD)
                    link(v.tensor_tensor(heads(rot_a[:, :, :]), heads(part), r, ALU.mult))
                if kind == "spin_q":
                    turned(q_cols, 0, NH)
                if kind == "spin_k":
                    turned(k_cols, 1, NKV)
                    v.tensor_tensor(rot_b[:, :, q_cols], rot_b[:, :, q_cols], rot_a[:, :, q_cols], ALU.add)
                    v.tensor_tensor(k_rot[:, :, :], rot_b[:, :, k_cols], rot_a[:, :, k_cols], ALU.add).then_inc(s_roped, 1)
                if kind in ("qT", "kT"):
                    p, pieces, rows = (full(), q_pieces, P) if kind == "qT" else (full(), k_pieces, NKV * HD)
                    if kind == "qT":
                        wait(dve, s_stored, 16 * STORES * (2 * b + half))
                    p, left = p[0:rows, :], rest[0:rows, :]
                    link(v.tensor_copy(pieces[:, 0, :], p))
                    v.tensor_tensor(left, p, pieces[:, 0, :], ALU.subtract).then_inc(s_bank_free, 1)
                    dve.wait_ge(s_bank_free, use["base"] + use["n"])
                if kind in ("qT2", "kT2"):
                    pieces, rows = (q_pieces, P) if kind == "qT2" else (k_pieces, NKV * HD)
                    left = rest[0:rows, :]
                    link(v.tensor_copy(pieces[:, 1, :], left))
                    v.tensor_tensor(pieces[:, 2, :], left, pieces[:, 1, :], ALU.subtract).then_inc(s_split, 1)

            def evacuate(b, qb, k):
                g = slot_base(b, qb) + (k + 1) * KB_OF[qb]
                dve.wait_ge(s_pv, g)
                v.tensor_copy(o_sb[:, k % 2, :], o_ps[:, :]).then_inc(s_o, 1)

            def keep_y(unit, q):
                n = quarter_steps(q)
                dve.wait_ge(s_h1_used, STEPS * unit + q * TU + n)
                dve.wait_ge(s_y_stored[q % 2], 16 * (QUARTERS // 2 * unit + q // 2 + 1))
                v.tensor_copy(y_sb[:, q % 2, 0:n, :], y_ps[:, 0:n, :]).then_inc(s_y_free, 1)

            def finish(item, own_b, own_qb):
                kind, which, back = item
                b, qb, unit = unit_of(own_b, own_qb, back)
                res = x_all[:, ds(b * TB + qb * TU, TU), :]
                if kind == "turn":
                    k, p = which, full()
                    o = p.rearrange("p (t h r) -> p t h r", t=TU, h=REP)
                    link(v.reciprocal(den[:, :, :], o[:, :, :, HD]))
                    d = spread(den[:, :, :].rearrange("p t (h a) -> p t h a", a=1), 3, HD)
                    to = o_tok[:, :, k * REP * HD:(k + 1) * REP * HD].rearrange("p t (h d) -> p t h d", d=HD)
                    v.tensor_tensor(to, o[:, :, :, 0:HD], d, ALU.mult).then_inc(s_bank_free, 1)
                if kind == "oT":
                    v.tensor_copy(o_t[:, :], full()).then_inc(s_bank_free, 1)
                if kind == "wo":
                    p = full()
                    ga = spread(gates[:, ds(b, 1), 0, :], 1, TU)
                    v.tensor_tensor(attn[:, :, :], p.rearrange("p (t d) -> p t d", t=TU), ga, ALU.mult) \
                        .then_inc(s_bank_free, 1)
                    dve.wait_ge(s_bank_free, use["base"] + use["n"])
                    link(v.tensor_tensor(res, res, attn[:, :, :], ALU.add), plain=True)
                if kind == "stat2":
                    for t in range(TU):
                        last = v.bn_stats(stats2[:, t, :], x_all[:, ds(b * TB + qb * TU + t, 1), :])
                    link(last, plain=True)
                    for t in range(TU):
                        last = v.bn_aggr(mean_var2[:, t, :], stats2[:, t, :])
                    link(last)
                if kind == "root2":
                    link(v.tensor_scalar(var_e[:, :], mean_var2[:, :, 1], LN_EPS, None, ALU.add))
                    rsqrt(rstd2[:, :], var_e[:, :], TU)
                if kind == "xn2":
                    wait(dve, s_scattered, 16 * 2 * TU * unit)
                    for t in range(TU):
                        last = v.tensor_scalar(xn2[:, t, :], x_all[:, ds(b * TB + qb * TU + t, 1), :],
                                               mean_var2[:, t, 0:1], rstd2[:, t:t + 1], ALU.subtract, ALU.mult)
                    last.then_inc(s_xn2, 1)
                    dve.wait_ge(s_xn2, unit + 1)
                s, m, r, over, sg = (pick_f[:, i, :] for i in range(5))
                if kind == "pick":
                    first2 = [spread(mod_pick[:, ds(b, 1), i, :], 1, TU) for i in (1, 0)]
                    link(v.tensor_tensor(pick[:, :, :], xn2[:, :, 0:2], first2[0], ALU.mult))
                    link(v.tensor_tensor(pick[:, :, :], pick[:, :, :], first2[1], ALU.add))
                    link(v.tensor_tensor(s, pick[:, :, 0], pick[:, :, 1], ALU.add))
                    link(v.tensor_scalar(m, s, -1.0, None, ALU.mult))
                    link(v.tensor_tensor(m, m, s, ALU.max))
                    link(v.tensor_copy(pick_i[:, 0, :], m))
                    link(v.tensor_copy(r, pick_i[:, 0, :]))
                if kind == "pick2":
                    link(v.tensor_tensor(over, r, m, ALU.is_gt))
                    link(v.tensor_tensor(r, r, over, ALU.subtract))
                    link(v.tensor_scalar(sg, s, 0.0, 2.0, ALU.is_ge, ALU.mult))
                    link(v.scalar_tensor_tensor(out=r, in0=sg, scalar=-1.0, in1=r, op0=ALU.add, op1=ALU.mult))
                    link(v.tensor_copy(pick_i[:, 0, :], r))
                    link(v.tensor_scalar(pick_i[:, 1, :], pick_i[:, 0, :], NE - 1, None, ALU.bitwise_and))
                    h = spread(pick_i[:, 1, :].rearrange("p (t a) -> p t a", a=1), 2, NE)
                    link(v.tensor_tensor(near[:, :, :], expert[:, :, :], h, ALU.subtract))
                    link(v.tensor_scalar(near[:, :, :], near[:, :, :], NE - 1, None, ALU.bitwise_and))
                    v.tensor_scalar(w8[:, qb, :, :], near[:, :, :], 1.0, 0.5, ALU.is_le, ALU.mult).then_inc(s_w8, 1)
                if kind == "rank":
                    v.tensor_copy(rank[:, :, :, :].rearrange("p i t e -> p (i t e)"), full()[:, 0:2 * TU * NE]) \
                        .then_inc(s_bank_free, 1)
                    dve.wait_ge(s_bank_free, use["base"] + use["n"])
                    for t in range(1, TU):
                        link(v.tensor_tensor(rank[:, 1, t, :], rank[:, 1, t, :], rank[:, 1, t - 1, :], ALU.add))
                    link(v.tensor_tensor(rank[:, 0, 1:TU, :], rank[:, 0, 1:TU, :], rank[:, 1, 0:TU - 1, :], ALU.add))
                    link(v.tensor_scalar(n_steps_i[:, :], rank[:, 1, TU - 1, :], float(P - 1), None, ALU.add))
                    link(v.tensor_scalar(n_steps_i[:, :], n_steps_i[:, :], P.bit_length() - 1, None, ALU.logical_shift_right))
                    link(v.tensor_copy(n_steps[:, :], n_steps_i[:, :]))
                    each = spread(n_steps[:, :].rearrange("p (a e) -> p a e", a=1), 1, NE)
                    link(v.tensor_tensor(up_to_n[:, :, :], up_to[:, :, :], each, ALU.mult))
                    link(v.tensor_reduce(ends[:, :], up_to_n[:, :, :], AX.X, ALU.add))
                    link(v.tensor_tensor(starts[:, :], ends[:, :], n_steps[:, :], ALU.subtract))
                if kind == "place":
                    first = spread(starts[:, :].rearrange("p (a e) -> p a e", a=1), 1, TU)
                    link(v.scalar_tensor_tensor(out=rank[:, 0, :, :], in0=first, scalar=float(P), in1=rank[:, 0, :, :],
                                                op0=ALU.mult, op1=ALU.add))
                    for j in range(2):
                        last = v.scalar_tensor_tensor(out=place_of[:, j, :, :], in0=near[:, :, :], scalar=float(j),
                                                      in1=rank[:, 0, :, :], op0=ALU.is_equal, op1=ALU.mult)
                    link(last)
                    link(v.tensor_reduce(place_f[:, :, :].rearrange("p j t -> p (j t)"),
                                         place_of[:, :, :, :].rearrange("p j t e -> p (j t) e"), AX.X, ALU.add))
                    v.tensor_copy(place[:, qb, :, :], place_f[:, :, :]).then_inc(s_place, 1)
                if kind == "steps":
                    end = spread(ends[:, :].rearrange("p (a e) -> p a e", a=1), 1, QUARTERS * TU)
                    link(v.tensor_tensor(over_end[:, :, :], end, step_no[:, :, :], ALU.is_le))
                    link(v.tensor_reduce(of_step[:, :], over_end[:, :, :], AX.X, ALU.add))
                    link(v.tensor_scalar(of_step[:, :], of_step[:, :], float(NE - 1), float(P), ALU.min, ALU.mult))
                    v.tensor_scalar(w_row[:, qb, :], of_step[:, :], row_no[:, 0:1], None, ALU.add).then_inc(s_w_row, 1)
                if kind == "hsT":
                    q, w = which, quarter_steps(which) * P
                    p = full()
                    wait(dve, s_h1_used, STEPS * unit + ((q - 1) * TU if q >= 2 else (QUARTERS - 1) * TU - STEPS if q == 0 else 0))
                    v.tensor_scalar(h2_t[:, q % 2, 0:w], p[:, 0:w], mod_t[:, 4, ds(b, 1)], mod_t[:, 3, ds(b, 1)],
                                    ALU.mult, ALU.add).then_inc(s_bank_free, 1)
                    dve.sem_inc(s_turned, 1)
                if kind == "w8":
                    v.tensor_copy(w8_t[:, :], full()[0:NE, :]).then_inc(s_bank_free, 1)
                if kind == "b2":
                    p = full()
                    dve.wait_ge(s_gathered, 16 * 2 * TU * (unit + 1))
                    y0, y1 = y_tok[:, 0, :, :], y_tok[:, 1, :, :]
                    link(v.tensor_tensor(y0, y0, y1, ALU.add))
                    v.scalar_tensor_tensor(out=y0, in0=y0, scalar=0.5, in1=p.rearrange("p (t d) -> p t d", t=TU),
                                           op0=ALU.mult, op1=ALU.add).then_inc(s_bank_free, 1)
                    dve.wait_ge(s_bank_free, use["base"] + use["n"])
                    gb = spread(gates[:, ds(b, 1), 1, :], 1, TU)
                    link(v.tensor_tensor(y0, y0, gb, ALU.mult))
                    v.tensor_tensor(res, res, y0, ALU.add).then_inc(s_sum, 1)
                if kind == "ffn":
                    u, p = which, full()
                    if u < 2:
                        wait(dve, s_h1_used, STEPS * unit)
                    else:
                        dve.wait_ge(s_h1_used, STEPS * unit + u - 1)
                    for ch in range(NC):
                        last = v.tensor_scalar(h1[:, u % 2, ch, :], p[:, ch * P:(ch + 1) * P],
                                               w_ring[:, u % WRING, 2 * DFF + ch:2 * DFF + ch + 1], 0.0, ALU.add, ALU.max)
                    last.then_inc(s_bank_free, 1)
                    if u and u % TU == 0:
                        keep_y(unit, u // TU - 1)
                if kind == "end":
                    keep_y(unit, QUARTERS - 1)

            def phase(b, qb, kind, i=0):
                begin(kind, qb, i)
                items = PLAN[kind, qb]
                before = (b, 0) if qb else (b - 1, 1)
                nkb = KB_OF[qb]
                for l in range(SLOTS_OF[qb]):
                    for item in items[l]:
                        if item[0] in PREP:
                            prep(item, b, qb)
                        else:
                            finish(item, b, qb)
                    if l == 0 and (kind, qb) != ("first", 0):
                        evacuate(*before, NKV - 1)
                    elif l and l % nkb == 0:
                        evacuate(b, qb, l // nkb - 1)

            dve.wait_ge(s_const, CONSTS)
            v.tensor_copy(step_no[:, :, :], step_i[:, :, :])
            link(v.tensor_copy(row_no[:, :], row_i[:, :]))
            dve.wait_ge(s_x0, 16)
            for item in prep_items(0):
                prep(item, 0, 0)
            for b in range(NB):
                p = full()
                v.tensor_copy(gates[:, b, 0, :], p[:, 0:D])
                v.tensor_copy(gates[:, b, 1, :], p[:, 3 * D:4 * D])
                v.tensor_copy(mod_pick[:, b, 0, :], p[:, D:D + 2])
                v.tensor_scalar(mod_pick[:, b, 1, :], p[:, 2 * D:2 * D + 2], 1.0, None, ALU.add).then_inc(s_bank_free, 1)
                dve.wait_ge(s_bank_free, use["base"] + use["n"])
            for b in range(0, NB, 2):
                g = gates[:, b:b + 2, :, :].rearrange("p b i d -> p (b i d)")
                size = y_tok[:, 0, :, :].rearrange("p t d -> p (t d)")
                link(v.scalar_tensor_tensor(out=size, in0=g, scalar=-1.0, in1=g, op0=ALU.mult, op1=ALU.max))
                link(v.tensor_scalar(size, size, 0.25, None, ALU.max))
                link(v.tensor_scalar(g, g, 0.0, 2.0, ALU.is_ge, ALU.mult))
                link(v.scalar_tensor_tensor(out=g, in0=g, scalar=-1.0, in1=size, op0=ALU.add, op1=ALU.mult))
            dve.wait_ge(s_x, 16)
            phase(0, 0, "first")
            dve.wait_ge(s_h_zero, 32)
            phase(0, 1, "first")
            before_loop = chain["n"]
            with dve.Fori(0, NB - 2) as i:
                chain.update(base=before_loop + i * CHAIN_LOOP, n=0)
                for qb in range(2):
                    phase(i + 1, qb, "mid", i)
                chain_counts["loop"] = chain["n"]
            chain.update(base=before_loop + (NB - 2) * CHAIN_LOOP, n=0)
            for qb in range(2):
                phase(NB - 1, qb, "last")
            evacuate(NB - 1, 1, NKV - 1)
            begin("tail")
            for item in PLAN_TAIL:
                finish(item, NB, 0)


def rope_tables():
    inv = (np.float32(1.0) / np.float32(10000.0) ** (np.arange(0, HD, 2, dtype=np.float32) / np.float32(HD))).astype(np.float32)
    angle = np.outer(np.arange(SEQ, dtype=np.float32), inv).astype(np.float32)
    angle = np.concatenate([angle, angle], axis=-1)
    sign = np.where(np.arange(HD) < HD // 2, -1.0, 1.0).astype(np.float32)
    return np.stack([np.cos(angle), np.sin(angle) * sign]).astype(np.float32)


def kernel(**inputs):
    import concourse.bacc as bacc
    from concourse.bass_utils import run_bass_kernel_spmd

    nc = bacc.Bacc("TRN2", target_bir_lowering=False, num_devices=1)
    given = {n.removeprefix("L0_"): np.asarray(a) for n, a in inputs.items()}
    arrays = {
        "x": given["attn_x"],
        "wqkv": np.concatenate([given["attn_Wq"], given["attn_Wk"], given["attn_Wv"]]).T,
        "wo": given["attn_Wo"].T,
        "q_w": given["attn_q_norm_w"],
        "k_w": given["attn_k_norm_w"],
        "weights": np.concatenate([
            given["ffn_W1"],
            given["ffn_W2"].reshape(NE, NC, P, D).transpose(0, 2, 1, 3).reshape(NE, P, NC * D),
            given["ffn_b1"].reshape(NE, NC, P).transpose(0, 2, 1)], axis=2).reshape(NE * P, WROW),
        "b2": given["ffn_b2"],
        "c": given["c"].T,
        "wmod": given["wmod"],
        "rope": rope_tables(),
    }
    arrays = {f"in_{n}": np.ascontiguousarray(a) for n, a in arrays.items()}
    args = [nc.dram_tensor(n, a.shape, mybir.dt.from_np(a.dtype), kind="ExternalInput").ap() for n, a in arrays.items()]
    args.append(nc.dram_tensor("out", (NB, SEQ, D), F32, kind="ExternalOutput").ap())
    counts = {}
    adaln_block(nc, *args, counts)
    assert counts["loop"] == CHAIN_LOOP, counts
    r = run_bass_kernel_spmd(nc, [arrays], core_ids=[0])
    return r.results[0]["out"]
```

```python
from contextlib import ExitStack

import numpy as np

import concourse.bass as bass
from concourse import mybir

ALU = mybir.AluOpType
ACT = mybir.ActivationFunctionType
F32 = mybir.dt.float32
BF16 = mybir.dt.bfloat16
I32 = mybir.dt.int32
AX = mybir.AxisListType

P = 128
NB, SEQ, D = 4, 1024, 128
NH, NKV, HD = 16, 4, 8
REP = NH // NKV
NQK = NH + NKV
NE, DFF = 8, 512
NC = DFF // P
QB = 512
TU = QB // P
TB = SEQ // P
NPIECE = 3
KR = NPIECE * NPIECE * HD
CAP = 30.0
SCALE = float(HD) ** -0.5
LN_EPS, RMS_EPS = 1e-5, 1e-6
QKVW = (NH + 2 * NKV) * HD
VW = 32
RING = 4
LAG = 2

KB_OF = (TU, 2 * TU)
SLOTS_OF = (NKV * KB_OF[0], NKV * KB_OF[1])
SLOTS = sum(SLOTS_OF)
assert SLOTS % RING == 0 and SLOTS_OF[0] % RING == 0

SETUP_USES = 1 + NB
PREP = ["stat", "root", "root b", "root c", "xn", "lnT", "qkv0", "qkv1", "square", "rms", "rroot", "rroot b", "rroot c",
        "heads", "spin_q", "spin_k", "qT", "qT2", "kT", "kT2"]
WITH_BANK = {"lnT", "qkv0", "qkv1", "qT", "kT", "turn", "oT", "wo", "rank", "hsT", "ffn"}

STEPS = (2 * QB + NE * (P - 1)) // P
QUARTERS = -(-STEPS // TU)
WROW = 2 * DFF + NC + D
WRING = 4
LEAD = 2
NOW, NEXT = 6, 14


def prep_items(back):
    return [(what, 0, back) for what in PREP]


CHAIN = ["oT", "wo", "stat2", "root2", "root2 b", "root2 c", "xn2", "pick", "pick2", "rank", "place", "steps"]


def slot_shape(qb, l):
    kv, kb = divmod(l, KB_OF[qb])
    d = kb - TU * qb
    return kv, kb, max(d, 0) * P, d >= 0


def quarter_steps(q):
    return min(TU, STEPS - TU * q)


def experts(steps, following):
    out = []
    ahead = steps + following
    for j, (u, back) in enumerate(steps):
        items = []
        if u == 0 and j == 0:
            items.append(("hsT", 0, back))
        if u == STEPS - 1 and j + 1 < len(steps):
            items.append(("hsT", 0, steps[j + 1][1]))
        if (u + 1) % TU == 0 and u + 1 < STEPS:
            items.append(("hsT", (u + 1) // TU, back))
        items.append(("ffn", u, back))
        if j + LEAD < len(ahead):
            items.append(("weights", *ahead[j + LEAD]))
        if u == STEPS - 1:
            items.append(("end", 0, back))
        out.append(items)
    return out


EARLY = [(u, 2) for u in range(NOW, NEXT)]
LATE = [(u, 3) for u in range(NEXT, STEPS)] + [(u, 2) for u in range(STEPS)] \
    + [(u, 1) for u in range(NOW)]
LATEST = LATE[:-NOW] + [(u, 1) for u in range(STEPS)]
FIRST = [(u, 1) for u in range(NOW)]
TAIL = [(u, 1) for u in range(STEPS)]


def shift(steps):
    return [(u, back - 1) for u, back in steps[:LEAD]]


SCHEDULE = {
    ("first", 0): {
        "ahead": [1, 1, 1, 1, 1, 1, 1.5, 5, 5, 5.5, 6.0, 6.0, 6.0, 6.0, 6.0, 7.0, 9.0, 10.0, 10.5, 10.5],
        "stacks": [14.75],
        "v": [12.25],
        "values": [4, 3, 3, 99, 0, 1, 4, 2, 99, 99, 99, 1, 99, 0, 0, 2],
    },
    ("mid", 0): {
        "stacks": [9.5],
        "v": [6.0],
        "chain": [2, 2, 2, 2.5, 2.5, 3, 3, 4.75, 5, 6, 7.5, 8.25, 8.25, 8.25, 8.25, 11.0, 11.5, 12.25],
        "steps": [0.5, 1.0, 3.5, 4.5, 6, 9, 13.75, 15],
        "values": [99, 99, 1, 99, 3, 4, 3, 99, 99, 2, 1, 3, 0, 99, 99, 4],
    },
    ("last", 0): {
        "stacks": [8.5],
        "v": [6.5],
        "chain": [2, 2, 2, 2.5, 2.5, 3, 3, 4.75, 5, 6, 7.5, 8.25, 8.25, 8.25, 8.25, 11.0, 11.5, 12.25],
        "steps": [0, 1.0, 3.5, 4.5, 6, 9, 13.75, 15],
        "values": [99, 99, 1, 99, 3, 4, 3, 99, 99, 2, 1, 3, 0, 99, 99, 4],
    },
    ("mid", 1): {
        "ahead": [2, 3, 3, 3, 3, 4, 5, 5, 6, 7, 8, 9, 9, 9, 10.25, 10.5, 12, 13, 13, 14, 15.5, 16, 16, 17,
            17, 18, 18.75, 20, 21.0, 21.0, 22.5, 22.5, 22.5, 22.5, 23, 24.5, 26.5, 26.5, 28, 28.5],
        "stacks": [27.25],
        "v": [24.25],
        "chain": [2, 2.5, 3, 4, 4, 4, 4, 5.0, 5.0, 10.0, 10.0, 10.5, 10.5, 10.5, 13.25, 17.5, 18.5, 20.0],
        "back": [2.0, 2.5, 3.5, 5, 7, 22, 26.25, 26.5, 26.5, 30],
        "steps": [0, 1, 3, 5.25, 5.5, 7, 9, 10, 11, 12, 14, 16, 17.5, 18, 19, 21, 23, 25, 26, 27, 28.5,
            30.5],
        "values": [2, 99, 3, 3, 3, 2, 3, 99, 3, 1, 99, 2, 2, 4, 99, 4, 99, 99, 0, 2, 2, 99, 3, 1, 3, 99, 99,
            99, 99, 99, 99, 2],
    },
    ("first", 1): {
        "ahead": [2, 3, 3, 3, 3, 4, 5, 5, 9, 10, 11.5, 11.5, 11.5, 11.5, 12, 13, 13, 13, 13, 14, 16, 16, 16,
            16, 17, 18, 19, 20, 20, 21, 25, 25, 25, 25, 25, 26, 27, 27, 28, 29],
        "stacks": [26.25],
        "v": [26.0],
        "chain": [2, 2, 3, 7, 9.5, 9.5, 9.5, 9.5, 9.5, 9.5, 9.5, 11, 11, 15.75, 17.25, 17.25, 18, 19],
        "weights": [16.75, 20.75],
        "steps": [21, 25, 25, 26.75, 28.5, 29.5],
        "values": [1, 0, 4, 1, 2, 4, 4, 1, 1, 4, 1, 99, 0, 0, 99, 0, 3, 1, 2, 0, 3, 99, 99, 99, 4, 99, 1, 2,
            4, 99, 99, 99],
    },
    ("last", 1): {
        "chain": [2, 2, 2, 2.5, 2.5, 2.75, 2.75, 3.5, 4.5, 4.5, 7.0, 7.5, 7.5, 9.0, 9.0, 9.25, 10.25, 12.5],
        "back": [3.5, 3.5, 3.5, 3.5, 6.0, 18.0, 18.0, 18.25, 18.75, 20.25],
        "steps": [0, 1, 2, 2, 3, 4, 6.5, 7, 8, 9, 10, 11, 11, 12.5, 13, 15, 15, 17.75, 18.5, 19, 19.5,
            20.25, 21.25, 23.25, 24.5, 25, 26, 27.25, 27.25, 28.5, 30],
        "values": [99, 99, 99, 99, 4, 99, 99, 1, 1, 1, 3, 4, 0, 0, 3, 4, 1, 3, 4, 99, 3, 4, 0, 0, 0, 0, 99,
            0, 99, 4, 1, 1],
    },
}


def plan(kind, qb):
    nkb, n = KB_OF[qb], SLOTS_OF[qb]
    table = SCHEDULE[kind, qb]
    streams = {
        "ahead": prep_items(-1) + (prep_items(-2) if qb else []),
        "stacks": [("stacks", 0, -1)],
        "v": [("v", 0, -1)],
        "back": [i for back in (3, 2) for i in [("gather", t, back) for t in range(TU)] + [("sum", 0, back)]],
        "chain": [("turn", NKV - 1, 1)] + [(what, 0, 1) for what in CHAIN]
        + [("scatter", t, 1) for t in range(TU)] + [("sorted", 0, 1)],
        "weights": [("weights", u, 1) for u in range(LEAD)],
        "steps": experts(*STEPS_IN[kind, qb]),
    }
    put = [((k + 1) * nkb + LAG, [("turn", k, 0)]) for k in range(NKV - 1)]
    for name, items in streams.items():
        if name in table:
            assert len(table[name]) == len(items)
            put += [(at, item if name == "steps" else [item]) for at, item in zip(table[name], items)]
    put.sort(key=lambda x: x[0])
    return [[item for at, items in put if int(at) == slot for item in items] for slot in range(n)]


STEPS_IN = {
    ("first", 0): ([], []), ("first", 1): (FIRST, shift(EARLY)),
    ("mid", 0): (EARLY, shift(LATE)), ("mid", 1): (LATE, shift(EARLY)),
    ("last", 0): (EARLY, shift(LATE)), ("last", 1): (LATEST, []),
}
PLAN = {(kind, qb): plan(kind, qb) for kind in ("first", "mid", "last") for qb in range(2)}


def tail():
    out = [("gather", t, 2) for t in range(TU)] + [("turn", NKV - 1, 1)] + [(what, 0, 1) for what in CHAIN]
    out += [("scatter", t, 1) for t in range(TU)] + [("sorted", 0, 1)] + [("weights", u, 1) for u in range(LEAD)]
    out.append(("sum", 0, 2))
    for items in experts(TAIL, []):
        out += items
    return out + [("gather", t, 1) for t in range(TU)] + [("last sum", 0, 1)]


PLAN_TAIL = tail()
for phase_of, u in ((("first", 1), (NOW - 1, 1)), (("mid", 0), (NEXT - 1, 2)), (("mid", 1), (NOW - 1, 1)),
                    (("last", 0), (NEXT - 1, 2))):
    banked = [i for slot in PLAN[phase_of] for i in slot if i[0] in WITH_BANK]
    assert banked[-1] == ("ffn", *u)


def uses(items):
    return sum(i[0] in WITH_BANK for i in items)


def uses_of(p):
    return sum(uses(s) for s in p)


USES_SETUP = SETUP_USES + uses(prep_items(0))
USES = {kind: uses_of(PLAN[kind, 0]) + uses_of(PLAN[kind, 1]) for kind in ("first", "mid", "last")}
assert USES["mid"] % 2 == 0


def use_base(kind, qb, i):
    if kind == "setup":
        return 0
    base = USES_SETUP + (uses_of(PLAN[kind, 0]) if qb == 1 else 0)
    if kind == "mid":
        base += USES["first"] + i * USES["mid"]
    if kind in ("last", "tail"):
        base += USES["first"] + (NB - 2) * USES["mid"] + (USES["last"] if kind == "tail" else 0)
    return base


def slot_base(b, qb):
    return b * SLOTS + qb * SLOTS_OF[0]


def diagonals(qb, l):
    return sum(slot_shape(qb, i)[3] for i in range(l))


def unit_of(b, qb, back):
    half = (qb - back) % 2
    return b - (back - qb + half) // 2, half, 2 * b + qb - back


def spread(ap, axis, n):
    shape = list(ap.shape)
    assert shape[axis] == 1
    shape[axis] = n
    return ap.broadcast_to(tuple(shape))


def wait(eng, sem, value):
    if isinstance(value, int) and value <= 0:
        return
    eng.wait_ge(sem, value)


def adaln_block(nc, x, wqkv, wo, q_w, k_w, weights, c, wmod, rope, out):
    ctx = ExitStack()
    with ctx:
        def sb(name, shape, dt=F32):
            return ctx.enter_context(nc.sbuf_tensor(name, shape, dt))

        def ps(name, shape, dt=F32):
            return ctx.enter_context(nc.psum_tensor(name, shape, dt))

        def sem(name):
            return ctx.enter_context(nc.semaphore(name))

        x_all = sb("x_all", [P, NB * TB, D])
        w_ring = sb("w_ring", [P, WRING, WROW])
        wqkv_t = sb("wqkv_t", [P, QKVW])
        wo_t = sb("wo_t", [P, D])
        c_t = sb("c_t", [P, NB])
        silu_w = sb("silu_w", [P, 3, NB])
        mod_t = sb("mod_t", [P, 6, NB])
        gates = sb("gates", [P, NB, 2, D])
        mod_pick = sb("mod_pick", [P, NB, 2, 2])
        ident = sb("ident", [P, P])
        expert = sb("expert", [P, TU, NE], I32)
        rope_sb = sb("rope_sb", [P, 2, TB, HD])
        qk_w = sb("qk_w", [P, 2, HD])
        rope_w = sb("rope_w", [P, 2, 2, TB, HD])
        Q = [sb(f"q_stack{i}", [KR, NH, QB], BF16) for i in range(2)]
        K = [sb(f"k_stack{i}", [KR, i + 1, NKV, QB], BF16) for i in range(2)]
        V = [sb(f"v_pad{i}", [P, KB_OF[i], NKV, VW]) for i in range(2)]
        probs = sb("probs", [P, RING, REP, QB])
        early = probs[:, RING - 1, :, :].rearrange("p h q -> p (h q)")
        wmod_sb = early[:, 3 * D:9 * D]
        silu_bc = probs[:, RING - 2, 0, :].rearrange("p (b c) -> p b c", b=NB)
        stats = sb("stats", [P, TU, 6])
        mean_var = sb("mean_var", [P, TU, 2])
        rstd = sb("rstd", [P, TU])
        nw_a = sb("nw_a", [P, TU * NQK])
        nw_i = sb("nw_i", [P, TU * NQK], I32)
        var_e = sb("var_e", [P, TU])
        mean_sq = sb("mean_sq", [P, TU * NQK])
        rms = sb("rms", [P, TU * NQK])
        xn = sb("xn", [P, TU, D])
        h_t = sb("h_t", [P, QB])
        qkv = sb("qkv", [P, TB, QKVW])
        rot_a = sb("rot_a", [P, TU, NQK * HD])
        rot_b = sb("rot_b", [P, TU, NQK * HD])
        k_rot = sb("k_rot", [P, TU, NKV * HD])
        rest = sb("rest", [P, QB])
        q_pieces = sb("q_pieces", [P, NPIECE, QB], BF16)
        k_pieces = sb("k_pieces", [NKV * HD, NPIECE, QB], BF16)
        o_sb = sb("o_sb", [P, 2, QB])
        den = sb("den", [P, TU, REP])
        o_tok = sb("o_tok", [P, TU, D])
        o_t = sb("o_t", [P, QB])
        attn = sb("attn", [P, TU, D])
        xn2 = sb("xn2", [P, TU, D])
        stats2 = sb("stats2", [P, TU, 6])
        mean_var2 = sb("mean_var2", [P, TU, 2])
        var_e2 = sb("var_e2", [P, TU])
        rstd2 = sb("rstd2", [P, TU])
        pick = sb("pick", [P, TU, 2])
        pick_f = sb("pick_f", [P, 5, TU])
        pick_i = sb("pick_i", [P, 2, TU], I32)
        near = sb("near", [P, TU, NE], I32)
        w8 = sb("w8", [P, 2, TU, NE])
        before2 = sb("before2", [P, P])
        all2 = sb("all2", [P, P])
        up_to = sb("up_to", [P, NE, NE])
        step_i = sb("step_i", [P, QUARTERS * TU, NE], I32)
        step_no = sb("step_no", [P, QUARTERS * TU, NE])
        row_i = sb("row_i", [P, 1], I32)
        row_no = sb("row_no", [P, 1])
        rank = sb("rank", [P, 2, TU, NE])
        n_steps_i = sb("n_steps_i", [P, NE], I32)
        n_steps = sb("n_steps", [P, NE])
        up_to_n = sb("up_to_n", [P, NE, NE])
        ends = sb("ends", [P, NE])
        starts = sb("starts", [P, NE])
        place_of = sb("place_of", [P, 2, TU, NE])
        place_f = sb("place_f", [P, 2, TU])
        place = sb("place", [P, 2, 2, TU], I32)
        over_end = sb("over_end", [P, QUARTERS * TU, NE])
        of_step = sb("of_step", [P, QUARTERS * TU])
        w_row = sb("w_row", [P, 2, QUARTERS * TU], I32)
        h_sorted = sb("h_sorted", [P, STEPS, D])
        h2_t = sb("h2_t", [P, 2, QB])
        h1 = sb("h1", [P, 2, NC, P])
        y_sb = sb("y_sb", [P, 2, TU, D])
        y_tok = sb("y_tok", [P, 2, TU, D])

        scores = ps("scores", [P, REP, QB])
        o_ps = ps("o_ps", [P, QB])
        bank = ps("bank", [P, 2, QB])
        y_ps = ps("y_ps", [P, TU, D])

        q_dram = nc.dram_tensor("q_dram", (NB, 2, NPIECE, HD, NH, QB), BF16, kind="Internal").ap()
        k_dram = nc.dram_tensor("k_dram", (NB, 2, NPIECE, HD, NKV, QB), BF16, kind="Internal").ap()

        h_dram = [nc.dram_tensor(f"h_dram{i}", (STEPS * P, D), F32, kind="Internal").ap() for i in range(2)]
        y_dram = [nc.dram_tensor(f"y_dram{i}", (STEPS * P, D), F32, kind="Internal").ap() for i in range(2)]

        s_alone = sem("s_alone")
        s_c = sem("s_c")
        s_small = sem("s_small")
        s_x0 = sem("s_x0")
        s_x = sem("s_x")
        s_rope_in = sem("s_rope_in")
        s_const = sem("s_const")
        s_tables = sem("s_tables")
        s_exp0 = sem("s_exp0")
        s_silu = sem("s_silu")
        s_xn = sem("s_xn")
        s_chain = sem("s_chain")
        s_bank_full = sem("s_bank_full")
        s_bank_free = sem("s_bank_free")
        s_roped = sem("s_roped")
        s_split = sem("s_split")
        s_stored = [sem("s_stored_q"), sem("s_stored_k")]
        s_stack = [sem("s_stack0"), sem("s_stack1")]
        s_v = [sem("s_v0"), sem("s_v1")]
        s_scored = sem("s_scored")
        s_tanh = sem("s_tanh")
        s_exp = sem("s_exp")
        s_masked = sem("s_masked")
        s_pv = sem("s_pv")
        s_o = sem("s_o")
        s_xn2 = sem("s_xn2")
        s_w8 = sem("s_w8")
        s_place = sem("s_place")
        s_w_row = sem("s_w_row")
        s_zero = sem("s_zero")
        s_h_zero = sem("s_h_zero")
        s_scattered = sem("s_scattered")
        s_sorted = [sem(f"s_sorted{q}") for q in range(QUARTERS)]
        s_turned = sem("s_turned")
        s_weights = [sem(f"s_weights{i}") for i in range(WRING)]
        s_h1_used = sem("s_h1_used")
        s_y_free = sem("s_y_free")
        s_y_stored = [sem(f"s_y_stored{i}") for i in range(2)]
        s_gathered = sem("s_gathered")
        s_gathered_last = [sem(f"s_gathered_last{t}") for t in range(TU)]
        s_sum_last = sem("s_sum_last")
        s_sum = sem("s_sum")
        s_out = sem("s_out")

        def ds(i, n):
            return slice(i, i + n) if isinstance(i, int) else bass.ds(i, n)

        LOADS = (NPIECE + 1, NPIECE + 2)

        CONSTS = 14

        block = ctx.enter_context(nc.Block())

        @block.sync
        def _(sp):
            sp.dma_start(c_t[:, :], c).then_inc(s_c, 16)
            xt = x.rearrange("b (t p) d -> p (b t) d", p=P)
            sp.dma_start(x_all[:, 0:TU, :], xt[:, 0:TU, :]).then_inc(s_x0, 16)
            sp.dma_start(wmod_sb[:, :], wmod).then_inc(s_small, 16)
            sp.dma_start(wqkv_t[:, :], wqkv).then_inc(s_small, 16)
            sp.dma_start(wo_t[:, :], wo).then_inc(s_small, 16)
            sp.dma_start(rope_sb[:, :, :, :], rope.rearrange("f (t p) d -> p f t d", p=P)).then_inc(s_rope_in, 16)
            sp.dma_start(qk_w[:, 0, :], spread(q_w.rearrange("(a d) -> a d", a=1), 0, P)).then_inc(s_rope_in, 16)
            sp.dma_start(qk_w[:, 1, :], spread(k_w.rearrange("(a d) -> a d", a=1), 0, P)).then_inc(s_rope_in, 16)
            sp.dma_start(x_all[:, TU:, :], xt[:, TU:, :]).then_inc(s_x, 16)
            sp.wait_ge(s_zero, 1)
            for i in range(2):
                sp.dma_start(h_dram[i].rearrange("(s p) d -> p s d", p=P), spread(y_sb[:, 0, 0:1, :], 1, STEPS)) \
                    .then_inc(s_h_zero, 16)

            def store_pieces(b, half, of_k):
                sp.wait_ge(s_split, 2 * (2 * b + half) + 1 + of_k)
                sp.sem_inc(s_alone, 1)
                dst, src = ((q_dram, q_pieces), (k_dram, k_pieces))[of_k]
                for i in range(NPIECE):
                    rows = dst[ds(b, 1), half, i, :, :, :].rearrange("a d h t -> h (a d) t")
                    sp.dma_start(rows, src[:, i, :]).then_inc(s_stored[of_k], 16)

            def load_stacks(b, qb):
                wait(sp, s_scored, 2 * (slot_base(b, 0) if qb else slot_base(b, 0) - SLOTS_OF[1]))
                sp.sem_inc(s_alone, 1)
                sp.wait_ge(s_stored[0], 16 * NPIECE * (2 * b + qb + 1))
                sp.sem_inc(s_alone, 1)
                for i in range(NPIECE):
                    src = q_dram[ds(b, 1), qb, i, :, :, :].rearrange("a d h t -> a d (h t)")
                    rows = slice(i * NPIECE * HD, (i + 1) * NPIECE * HD)
                    sp.dma_start(Q[qb][rows, :, :], spread(src, 0, NPIECE)).then_inc(s_stack[qb], 16)
                sp.wait_ge(s_stored[1], 16 * NPIECE * (2 * b + qb + 1))
                sp.sem_inc(s_alone, 1)
                for half in range(qb + 1):
                    src = k_dram[ds(b, 1), half, :, :, :, :].rearrange("a j d h t -> a (j d) (h t)")
                    sp.dma_start(K[qb][:, half, :, :], spread(src, 0, NPIECE)).then_inc(s_stack[qb], 16)

            xo = out.rearrange("b (t p) d -> p (b t) d", p=P)

            def store_out(b, qb):
                sp.wait_ge(s_sum, 2 * b + qb + 2)
                sp.sem_inc(s_alone, 1)
                here = ds(b * TB + qb * TU, TU)
                sp.dma_start(xo[:, here, :], x_all[:, here, :]).then_inc(s_out, 16)

            def load_sorted(qb, unit):
                sp.wait_ge(s_scattered, 16 * 2 * TU * (unit + 1))
                sp.sem_inc(s_alone, 1)
                wait(sp, s_turned, QUARTERS * unit)
                sp.sem_inc(s_alone, 1)
                for q in range(QUARTERS):
                    here = slice(q * TU, q * TU + quarter_steps(q))
                    sp.dma_start(h_sorted[:, here, :], h_dram[qb].rearrange("(s p) d -> p s d", p=P)[:, here, :]) \
                        .then_inc(s_sorted[q], 16)

            def store_y(qb, unit, q):
                sp.wait_ge(s_y_free, STEPS * unit + q * TU + quarter_steps(q))
                sp.sem_inc(s_alone, 1)
                if q == 0:
                    wait(sp, s_sum, unit)
                    sp.sem_inc(s_alone, 1)
                n = quarter_steps(q)
                rows = y_dram[qb][q * TU * P:(q * TU + n) * P, :]
                sp.dma_start(rows.rearrange("(s p) d -> p s d", p=P), y_sb[:, q % 2, 0:n, :]).then_inc(s_y_stored[q % 2], 16)

            def do(item, b, qb):
                kind, which, back = item
                ub, uqb, unit = unit_of(b, qb, back)
                if kind in ("qT2", "kT2"):
                    store_pieces(ub, uqb, kind == "kT2")
                if kind == "stacks":
                    load_stacks(ub, uqb)
                if kind == "sorted":
                    load_sorted(uqb, unit)
                if kind == "ffn" and which and which % TU == 0:
                    store_y(uqb, unit, which // TU - 1)
                if kind == "end":
                    store_y(uqb, unit, QUARTERS - 1)
                if kind == "sum":
                    store_out(ub, uqb)
                if kind == "last sum":
                    for t in range(TU):
                        sp.wait_ge(s_sum_last, t + 1)
                        here = slice((NB - 1) * TB + TU + t, (NB - 1) * TB + TU + t + 1)
                        sp.dma_start(xo[:, here, :], x_all[:, here, :]).then_inc(s_out, 16)

            def phase(b, qb, kind):
                for slot in PLAN[kind, qb]:
                    for item in slot:
                        do(item, b, qb)

            for of_k in range(2):
                store_pieces(0, 0, of_k)
            load_stacks(0, 0)
            for qb in range(2):
                phase(0, qb, "first")
            with sp.Fori(0, NB - 2) as i:
                for qb in range(2):
                    phase(i + 1, qb, "mid")
            for qb in range(2):
                phase(NB - 1, qb, "last")
            for item in PLAN_TAIL:
                do(item, NB, 0)
            sp.wait_ge(s_out, 16 * (2 * NB - 1 + TU))

        @block.gpsimd
        def _(pool):
            own = [0]

            def done(ins):
                own[0] += 1
                ins.then_inc(s_const, 1)

            done(nc.gpsimd.memset(ident[:, :], 0.0))
            done(nc.gpsimd.iota(expert[:, :, :], pattern=[[0, TU], [1, NE]], base=0, channel_multiplier=0))
            done(nc.gpsimd.iota(step_i[:, :, :], pattern=[[1, QUARTERS * TU], [0, NE]], base=0, channel_multiplier=0))
            done(nc.gpsimd.iota(row_i[:, :], pattern=[[0, 1]], base=0, channel_multiplier=1))
            done(nc.gpsimd.memset(before2[:, :], 2.0))
            done(nc.gpsimd.memset(all2[:, :], 2.0))
            done(nc.gpsimd.memset(up_to[:, :, :], 1.0))
            nc.gpsimd.memset(y_sb[:, 0, 0, :], 0.0).then_inc(s_zero, 1)
            for v in V:
                done(nc.gpsimd.memset(v[:, :, :, :], 0.0))
            pool.wait_ge(s_const, own[0])
            done(nc.gpsimd.affine_select(out=ident[:, :], in_=ident[:, :], compare_op=ALU.not_equal, fill=1.0, base=0,
                                         pattern=[[-1, P]], channel_multiplier=1))
            done(nc.gpsimd.affine_select(out=before2[:, :], in_=before2[:, :], compare_op=ALU.is_ge, fill=0.0, base=-1,
                                         pattern=[[1, P]], channel_multiplier=-1))
            done(nc.gpsimd.affine_select(out=up_to[:, :, :], in_=up_to[:, :, :], compare_op=ALU.is_ge, fill=0.0, base=0,
                                         pattern=[[1, NE], [-1, NE]], channel_multiplier=0))
            for v in V:
                done(nc.gpsimd.memset(v[:, :, :, HD:HD + 1], 1.0))
            pool.wait_ge(s_const, own[0])
            pool.wait_ge(s_rope_in, 48)
            for n in range(2):
                w = spread(qk_w[:, n:n + 1, :], 1, TB)
                nc.gpsimd.tensor_tensor(rope_w[:, 0, n, :, :], rope_sb[:, 0, :, :], w, ALU.mult).then_inc(s_tables, 1)
                for half in range(2):
                    here = slice(half * HD // 2, (half + 1) * HD // 2)
                    there = slice((1 - half) * HD // 2, (2 - half) * HD // 2)
                    nc.gpsimd.tensor_tensor(rope_w[:, 1, n, :, here], rope_sb[:, 1, :, here],
                                            w[:, :, there], ALU.mult).then_inc(s_tables, 1)
            def pad_values(b, qb):
                pool.wait_ge(s_roped, 2 * b + qb + 1)
                wait(pool, s_pv, slot_base(b, 0) if qb else slot_base(b, 0) - SLOTS_OF[1])
                pool.sem_inc(s_alone, 1)
                src = qkv[:, 0:KB_OF[qb], NQK * HD:].rearrange("p t (k d) -> p t k d", d=HD)
                nc.gpsimd.tensor_copy(V[qb][:, :, :, 0:HD], src).then_inc(s_v[qb], 1)

            def pool_wait(sem, value):
                wait(pool, sem, value)
                pool.sem_inc(s_alone, 1)

            def scatter(qb, unit, t):
                if t == 0:
                    pool_wait(s_xn2, unit + 1)
                    pool_wait(s_place, unit + 1)
                    for q in range(QUARTERS):
                        pool_wait(s_sorted[q], 16 * unit)
                for j in range(2):
                    to = bass.IndirectOffsetOnAxis(place[:, qb, j, t:t + 1], 0)
                    nc.gpsimd.indirect_dma_start(h_dram[qb], to, xn2[:, t, :], None).then_inc(s_scattered, 16)

            def load_weights(qb, unit, u):
                pool_wait(s_w_row, unit + 1)
                had = u - WRING if u >= WRING else max(range(u, STEPS, WRING)) - STEPS
                pool_wait(s_y_free, STEPS * unit + had + 1)
                row = bass.IndirectOffsetOnAxis(w_row[:, qb, u:u + 1], 0)
                nc.gpsimd.indirect_dma_start(w_ring[:, u % WRING, :], None, weights, row).then_inc(s_weights[u % WRING], 16)

            def gather(qb, unit, t):
                if t == 0:
                    for i in range(2):
                        pool_wait(s_y_stored[i], 16 * (QUARTERS // 2 * (unit + 1) + 1))
                    pool_wait(s_sum, unit + 1)
                for j in range(2):
                    at = bass.IndirectOffsetOnAxis(place[:, qb, j, t:t + 1], 0)
                    back = s_gathered_last[t] if isinstance(unit, int) and unit == 2 * NB - 1 else s_gathered
                    nc.gpsimd.indirect_dma_start(y_tok[:, j, t, :], None, y_dram[qb], at).then_inc(back, 16)

            def do(item, b, qb):
                kind, which, back = item
                ub, uqb, unit = unit_of(b, qb, back)
                if kind == "v":
                    pad_values(ub, uqb)
                if kind == "scatter":
                    scatter(uqb, unit, which)
                if kind == "weights":
                    load_weights(uqb, unit, which)
                if kind == "gather":
                    gather(uqb, unit, which)

            def phase(b, qb, items):
                for l in range(SLOTS_OF[qb]):
                    g = slot_base(b, qb) + l
                    kv, kb, off, diagonal = slot_shape(qb, l)
                    if diagonal:
                        pool.wait_ge(s_exp, g + 1)
                        pool.sem_inc(s_alone, 1)
                        tri = probs[:, l % RING, :, off:off + P]
                        nc.gpsimd.affine_select(out=tri, in_=tri, compare_op=ALU.is_ge, fill=0.0, base=0,
                                                pattern=[[0, REP], [1, P]], channel_multiplier=-1).then_inc(s_masked, 1)
                    for item in items[l]:
                        do(item, b, qb)

            for q in range(QUARTERS):
                pool.sem_inc(s_sorted[q], 16)
            pool.sem_inc(s_sum, 1)
            for i in range(2):
                pool.sem_inc(s_y_stored[i], 16)
            pad_values(0, 0)
            phase(0, 0, PLAN["first", 0])
            pool.wait_ge(s_h_zero, 32)
            phase(0, 1, PLAN["first", 1])
            with pool.Fori(0, NB - 2) as i:
                for qb in range(2):
                    phase(i + 1, qb, PLAN["mid", qb])
            for qb in range(2):
                phase(NB - 1, qb, PLAN["last", qb])
            for item in PLAN_TAIL:
                do(item, NB, 0)

        @block.scalar
        def _(act):
            act.wait_ge(s_c, 16)
            nc.scalar.activation(silu_w[:, 0, :], c_t[:, :], ACT.Exp, scale=-1.0).then_inc(s_exp0, 1)

            def cap(b, qb, l):
                g = slot_base(b, qb) + l
                _, _, off, _ = slot_shape(qb, l)
                r = l % RING
                wait(act, s_pv, g - RING + 1)
                if off < QB // 2:
                    for pair in range(2):
                        act.wait_ge(s_scored, 2 * g + pair + 1)
                        h = slice(2 * pair, 2 * pair + 2)
                        nc.scalar.activation(probs[:, r, h, off:QB], scores[:, h, off:QB], ACT.Tanh,
                                             scale=SCALE / CAP).then_inc(s_tanh, 1)
                else:
                    act.wait_ge(s_scored, 2 * g + 2)
                    nc.scalar.activation(probs[:, r, :, off:QB], scores[:, :, off:QB], ACT.Tanh,
                                         scale=SCALE / CAP).then_inc(s_tanh, 2)

            def exponential(b, qb, l):
                g = slot_base(b, qb) + l
                _, _, off, _ = slot_shape(qb, l)
                p = probs[:, l % RING, :, off:QB]
                act.wait_ge(s_tanh, 2 * g + 2)
                nc.scalar.activation(p, p, ACT.Exp, scale=CAP).then_inc(s_exp, 1)

            def phase(b, qb, last=False):
                n = SLOTS_OF[qb]
                for l in range(n):
                    if l + 1 < n:
                        cap(b, qb, l + 1)
                    elif not last:
                        cap(b + qb, 1 - qb, 0)
                    exponential(b, qb, l)

            cap(0, 0, 0)
            phase(0, 0)
            phase(0, 1)
            with act.Fori(0, NB - 2) as i:
                phase(i + 1, 0)
                phase(i + 1, 1)
            phase(NB - 1, 0)
            phase(NB - 1, 1, last=True)

        @block.tensor
        def _(pe):
            use = {}

            def begin(kind, qb=0, i=0):
                use.update(base=use_base(kind, qb, i), n=0, parity=use_base(kind, qb, 0) % 2)

            def take():
                n = use["base"] + use["n"]
                wait(pe, s_bank_free, n - 1)
                p = bank[:, (use["parity"] + use["n"]) % 2, :]
                use["n"] += 1
                return p, n

            def read_of(n):
                pe.wait_ge(s_bank_free, n + 1)

            def transposes(p, src_of, rows=P):
                for t in range(TU):
                    last = nc.tensor.transpose(p[0:rows, t * P:(t + 1) * P], src_of(t), ident[:, :])
                last.then_inc(s_bank_full, 1)

            begin("setup")
            pe.wait_ge(s_small, 16 * 3)
            pe.wait_ge(s_const, CONSTS)
            pe.wait_ge(s_silu, 1)
            p, _ = take()
            for i in range(6):
                last = nc.tensor.matmul(p[:, i * NB:(i + 1) * NB], wmod_sb[:, i * D:(i + 1) * D], silu_w[:, 2, :],
                                        start=True, stop=True)
            last.then_inc(s_bank_full, 1)
            def prep(item, own_b, own_qb, marks):
                kind = item[0]
                b, half, _ = unit_of(own_b, own_qb, item[2])
                if kind == "lnT":
                    pe.wait_ge(s_xn, 2 * b + half + 1)
                    p, n = take()
                    transposes(p, lambda t: xn[:, t, :])
                    marks[kind] = n
                if kind in ("qkv0", "qkv1"):
                    if kind == "qkv0":
                        read_of(marks["lnT"])
                    p, n = take()
                    for t in range(2):
                        i = 2 * (kind == "qkv1") + t
                        last = nc.tensor.matmul(p[:, t * QKVW:(t + 1) * QKVW], h_t[:, i * P:(i + 1) * P], wqkv_t[:, :],
                                                start=True, stop=True)
                    last.then_inc(s_bank_full, 1)
                if kind in ("qT", "kT"):
                    pe.wait_ge(s_roped, 2 * b + half + 1)
                    p, n = take()
                    if kind == "qT":
                        transposes(p, lambda t: rot_b[:, t, 0:NH * HD])
                    else:
                        transposes(p, lambda t: k_rot[:, t, :], rows=NKV * HD)

            def qk(b, qb, l):
                g = slot_base(b, qb) + l
                kv, kb, off, _ = slot_shape(qb, l)
                if l == 0:
                    pe.wait_ge(s_stack[qb], 16 * LOADS[qb] * (b + 1))
                for hh in range(REP):
                    if hh % 2 == 0:
                        wait(pe, s_tanh, 2 * (g - 1) + hh // 2 + 1)
                    last = nc.tensor.matmul(scores[:, hh, off:QB], K[qb][:, kb // TU, kv, kb % TU * P:(kb % TU + 1) * P],
                                            Q[qb][:, kv * REP + hh, off:QB], start=True, stop=True)
                    if hh % 2:
                        last.then_inc(s_scored, 1)

            def pv(b, qb, l):
                g = slot_base(b, qb) + l
                kv, kb, off, diagonal = slot_shape(qb, l)
                if l == 0:
                    pe.wait_ge(s_v[qb], b + 1)
                if kb == 0:
                    wait(pe, s_o, b * 2 * NKV + qb * NKV + kv)
                if diagonal:
                    pe.wait_ge(s_masked, b * 2 * NKV * TU + diagonals(0, qb * SLOTS_OF[0]) + diagonals(qb, l) + 1)
                else:
                    pe.wait_ge(s_exp, g + 1)
                for hh in range(REP):
                    last = nc.tensor.matmul(o_ps[32 * hh:32 * hh + VW, off:QB], V[qb][:, kb, kv, :],
                                            probs[:, l % RING, hh, off:QB], start=(kb == 0),
                                            stop=(kb == KB_OF[qb] - 1))
                last.then_inc(s_pv, 1)

            def finish(item, own_b, own_qb, marks):
                kind, which, back = item
                b, qb, unit = unit_of(own_b, own_qb, back)
                if kind == "turn":
                    k = which
                    pe.wait_ge(s_o, unit * NKV + k + 1)
                    p, n = take()
                    transposes(p, lambda t: o_sb[:, k % 2, t * P:(t + 1) * P])
                    marks[kind] = n
                if kind == "oT":
                    read_of(marks["turn"])
                    p, n = take()
                    transposes(p, lambda t: o_tok[:, t, :])
                    marks[kind] = n
                if kind == "wo":
                    read_of(marks["oT"])
                    p, n = take()
                    for t in range(TU):
                        last = nc.tensor.matmul(p[:, t * D:(t + 1) * D], o_t[:, t * P:(t + 1) * P], wo_t[:, :],
                                                start=True, stop=True)
                    last.then_inc(s_bank_full, 1)
                if kind == "rank":
                    pe.wait_ge(s_w8, unit + 1)
                    p, n = take()
                    tokens = w8[:, qb, :, :].rearrange("p t e -> p (t e)")
                    nc.tensor.matmul(p[:, 0:TU * NE], before2[:, :], tokens, start=True, stop=True)
                    nc.tensor.matmul(p[:, TU * NE:2 * TU * NE], all2[:, :], tokens, start=True, stop=True) \
                        .then_inc(s_bank_full, 1)
                if kind == "hsT":
                    pe.wait_ge(s_sorted[which], 16 * (unit + 2))
                    p, n = take()
                    for t in range(quarter_steps(which)):
                        last = nc.tensor.transpose(p[:, t * P:(t + 1) * P], h_sorted[:, which * TU + t, :], ident[:, :])
                    last.then_inc(s_bank_full, 1)
                    marks[kind, which] = n
                if kind == "ffn":
                    u, q = which, which // TU
                    if u % TU == 0:
                        read_of(marks["hsT", q])
                    pe.wait_ge(s_weights[u % WRING], 16 * (len(range(u % WRING, STEPS, WRING)) * unit + u // WRING + 1))
                    p, n = take()
                    for ch in range(NC):
                        last = nc.tensor.matmul(p[:, ch * P:(ch + 1) * P], w_ring[:, u % WRING, ch * P:(ch + 1) * P],
                                                h2_t[:, q % 2, u % TU * P:(u % TU + 1) * P], start=True, stop=True)
                    last.then_inc(s_bank_full, 1)
                    if u:
                        second(u - 1, unit, marks["ffn"])
                    marks["ffn"] = n
                if kind == "end":
                    second(STEPS - 1, unit, marks["ffn"])

            def second(u, unit, n):
                read_of(n)
                wait(pe, s_y_free, STEPS * unit + u)
                for ch in range(NC):
                    last = nc.tensor.matmul(y_ps[:, u % TU, :], h1[:, u % 2, ch, :],
                                            w_ring[:, u % WRING, DFF + ch * D:DFF + (ch + 1) * D],
                                            start=(ch == 0), stop=(ch == NC - 1))
                last.then_inc(s_h1_used, 1)

            def phase(b, qb, kind, i=0):
                begin(kind, qb, i)
                n, marks = SLOTS_OF[qb], dict(ffn=use["base"] - 1)
                items = PLAN[kind, qb]
                before = (b, 0) if qb else (b - 1, 1)
                for l in range(n):
                    if l + 1 < n:
                        qk(b, qb, l + 1)
                    elif (kind, qb) != ("last", 1):
                        qk(b + qb, 1 - qb, 0)
                    for j, item in enumerate(items[l] + [None]):
                        if j == min(SCHEDULE[kind, qb]["values"][l], len(items[l])):
                            if l >= LAG:
                                pv(b, qb, l - LAG)
                            elif (kind, qb) != ("first", 0):
                                pv(*before, SLOTS_OF[before[1]] + l - LAG)
                        if item and item[0] in PREP:
                            prep(item, b, qb, marks)
                        elif item:
                            finish(item, b, qb, marks)

            marks = {}
            for item in prep_items(0):
                if item[0] in WITH_BANK:
                    prep(item, 0, 0, marks)
            pe.wait_ge(s_silu, 2)
            for b in range(NB):
                p, _ = take()
                nc.tensor.matmul(p[:, :], silu_bc[:, b, :], wmod_sb[:, 2 * D:], start=True, stop=True).then_inc(s_bank_full, 1)
            assert use["n"] == USES_SETUP
            qk(0, 0, 0)
            phase(0, 0, "first")
            phase(0, 1, "first")
            with pe.Fori(0, NB - 2) as i:
                for qb in range(2):
                    phase(i + 1, qb, "mid", i)
            for qb in range(2):
                phase(NB - 1, qb, "last")
            for l in range(SLOTS_OF[1] - LAG, SLOTS_OF[1]):
                pv(NB - 1, 1, l)
            begin("tail")
            marks = {}
            for item in PLAN_TAIL:
                finish(item, NB, 0, marks)

        @block.vector
        def _(dve):
            v = nc.vector
            use, chain = {}, dict(n=0)

            def link(ins, plain=False):
                chain["n"] += 1
                ins.then_inc(s_chain, 1)
                dve.wait_ge(s_chain, chain["n"])
                if plain:
                    dve.sem_inc(s_alone, 1)

            def begin(kind, qb=0, i=0):
                use.update(base=use_base(kind, qb, i), n=0, parity=use_base(kind, qb, 0) % 2)

            def full():
                dve.wait_ge(s_bank_full, use["base"] + use["n"] + 1)
                p = bank[:, (use["parity"] + use["n"]) % 2, :]
                use["n"] += 1
                return p

            def rsqrt(y, val, n, first):
                a, i = nw_a[:, 0:n], nw_i[:, 0:n]
                if first:
                    link(v.tensor_scalar(i, val.bitcast(I32), 1, None, ALU.logical_shift_right))
                    link(v.tensor_scalar(y.bitcast(I32), i, -1.0, float(0x5F3759DF), ALU.mult, ALU.add))
                link(v.scalar_tensor_tensor(out=a, in0=y, scalar=-0.5, in1=y, op0=ALU.mult, op1=ALU.mult))
                link(v.tensor_tensor(a, a, val, ALU.mult))
                link(v.scalar_tensor_tensor(out=y, in0=a, scalar=1.5, in1=y, op0=ALU.add, op1=ALU.mult))

            begin("setup")
            dve.wait_ge(s_exp0, 1)
            link(v.tensor_scalar(silu_w[:, 1, :], silu_w[:, 0, :], 1.0, None, ALU.add))
            link(v.reciprocal(silu_w[:, 1, :], silu_w[:, 1, :]))
            v.tensor_tensor(silu_w[:, 2, :], c_t[:, :], silu_w[:, 1, :], ALU.mult).then_inc(s_silu, 1)
            dve.wait_ge(s_silu, 1)
            v.tensor_copy(silu_bc[:, :, :], spread(silu_w[:, 2, :].rearrange("p (b a) -> p b a", a=1), 2, P)).then_inc(s_silu, 1)
            def prep(item, own_b, own_qb):
                kind = item[0]
                b, half, _ = unit_of(own_b, own_qb, item[2])
                here = slice(half * TU, (half + 1) * TU)
                part = qkv[:, here, 0:NQK * HD]
                q_cols, k_cols, hh = slice(0, NH * HD), slice(NH * HD, NQK * HD), HD // 2

                def heads(ap):
                    return ap.rearrange("p t (h d) -> p t h d", d=HD)

                def table(f, n, count, cols=slice(0, HD)):
                    return spread(rope_w[:, f, n, here, cols].rearrange("p t (a d) -> p t a d", a=1), 2, count)

                def turned(src, n, count):
                    a, r = heads(rot_a[:, :, src]), heads(rot_b[:, :, src])
                    v.tensor_tensor(r[:, :, :, 0:hh], a[:, :, :, hh:], table(1, n, count, slice(0, hh)), ALU.mult)
                    link(v.tensor_tensor(r[:, :, :, hh:], a[:, :, :, 0:hh], table(1, n, count, slice(hh, HD)), ALU.mult))
                    link(v.tensor_tensor(a, a, table(0, n, count), ALU.mult))

                if kind == "stat":
                    dve.sem_inc(s_alone, 1)
                    for t in range(TU):
                        last = v.bn_stats(stats[:, t, :], x_all[:, ds(b * TB + half * TU + t, 1), :])
                    link(last, plain=True)
                    for t in range(TU):
                        last = v.bn_aggr(mean_var[:, t, :], stats[:, t, :])
                    link(last)
                if kind == "root":
                    link(v.tensor_scalar(var_e[:, :], mean_var[:, :, 1], LN_EPS, None, ALU.add))
                if kind in ("root", "root b", "root c"):
                    rsqrt(rstd[:, :], var_e[:, :], TU, kind == "root")
                if kind == "xn":
                    for t in range(TU):
                        last = v.tensor_scalar(xn[:, t, :], x_all[:, ds(b * TB + half * TU + t, 1), :],
                                               mean_var[:, t, 0:1], rstd[:, t:t + 1], ALU.subtract, ALU.mult)
                    last.then_inc(s_xn, 1)
                if kind == "lnT":
                    v.tensor_scalar(h_t[:, :], full(), mod_t[:, 1, ds(b, 1)], mod_t[:, 0, ds(b, 1)],
                                    ALU.mult, ALU.add).then_inc(s_bank_free, 1)
                if kind in ("qkv0", "qkv1"):
                    p, t0 = full(), half * TU + 2 * (kind == "qkv1")
                    if kind == "qkv0":
                        wait(dve, s_v[1], b)
                    v.tensor_copy(qkv[:, t0:t0 + 2, :], p[:, 0:2 * QKVW].rearrange("p (t n) -> p t n", t=2)) \
                        .then_inc(s_bank_free, 1)
                    dve.wait_ge(s_bank_free, use["base"] + use["n"])
                if kind == "square":
                    link(v.tensor_tensor(rot_a[:, :, :], part, part, ALU.mult))
                if kind == "rms":
                    link(v.tensor_reduce(mean_sq[:, :], rot_a[:, :, :].rearrange("p t (h d) -> p (t h) d", d=HD),
                                         AX.X, ALU.add))
                    link(v.tensor_scalar(mean_sq[:, :], mean_sq[:, :], 1.0 / HD, RMS_EPS, ALU.mult, ALU.add))
                if kind in ("rroot", "rroot b", "rroot c"):
                    rsqrt(rms[:, :], mean_sq[:, :], TU * NQK, kind == "rroot")
                if kind == "heads":
                    if isinstance(b, int) and b == 0 and half == 0:
                        dve.wait_ge(s_tables, 6)
                    r = spread(rms[:, :].rearrange("p (t h a) -> p t h a", t=TU, a=1), 3, HD)
                    link(v.tensor_tensor(heads(rot_a[:, :, :]), heads(part), r, ALU.mult))
                if kind == "spin_q":
                    turned(q_cols, 0, NH)
                if kind == "spin_k":
                    turned(k_cols, 1, NKV)
                    v.tensor_tensor(rot_b[:, :, q_cols], rot_b[:, :, q_cols], rot_a[:, :, q_cols], ALU.add)
                    v.tensor_tensor(k_rot[:, :, :], rot_b[:, :, k_cols], rot_a[:, :, k_cols], ALU.add).then_inc(s_roped, 1)
                if kind in ("qT", "kT"):
                    p, pieces, rows = (full(), q_pieces, P) if kind == "qT" else (full(), k_pieces, NKV * HD)
                    if kind == "qT":
                        wait(dve, s_stored[0], 16 * NPIECE * (2 * b + half))
                    else:
                        wait(dve, s_stored[1], 16 * NPIECE * (2 * b + half))
                    p, left = p[0:rows, :], rest[0:rows, :]
                    link(v.tensor_copy(pieces[:, 0, :], p))
                    v.tensor_tensor(left, p, pieces[:, 0, :], ALU.subtract).then_inc(s_bank_free, 1)
                    dve.wait_ge(s_bank_free, use["base"] + use["n"])
                if kind in ("qT2", "kT2"):
                    pieces, rows = (q_pieces, P) if kind == "qT2" else (k_pieces, NKV * HD)
                    left = rest[0:rows, :]
                    link(v.tensor_copy(pieces[:, 1, :], left))
                    v.tensor_tensor(pieces[:, 2, :], left, pieces[:, 1, :], ALU.subtract).then_inc(s_split, 1)

            def evacuate(b, qb, k):
                g = slot_base(b, qb) + (k + 1) * KB_OF[qb]
                dve.wait_ge(s_pv, g)
                v.tensor_copy(o_sb[:, k % 2, :], o_ps[:, :]).then_inc(s_o, 1)

            def keep_y(unit, u):
                q = u // TU
                dve.wait_ge(s_h1_used, STEPS * unit + u + 1)
                if u % TU == 0:
                    dve.wait_ge(s_y_stored[q % 2], 16 * (QUARTERS // 2 * unit + q // 2 + 1))
                v.tensor_tensor(y_sb[:, q % 2, u % TU, :], y_ps[:, u % TU, :], w_ring[:, u % WRING, WROW - D:], ALU.add) \
                    .then_inc(s_y_free, 1)

            def finish(item, own_b, own_qb):
                kind, which, back = item
                b, qb, unit = unit_of(own_b, own_qb, back)
                res = x_all[:, ds(b * TB + qb * TU, TU), :]
                if kind == "turn":
                    k, p = which, full()
                    o = p.rearrange("p (t h r) -> p t h r", t=TU, h=REP)
                    link(v.reciprocal(den[:, :, :], o[:, :, :, HD]))
                    d = spread(den[:, :, :].rearrange("p t (h a) -> p t h a", a=1), 3, HD)
                    to = o_tok[:, :, k * REP * HD:(k + 1) * REP * HD].rearrange("p t (h d) -> p t h d", d=HD)
                    v.tensor_tensor(to, o[:, :, :, 0:HD], d, ALU.mult).then_inc(s_bank_free, 1)
                if kind == "oT":
                    v.tensor_copy(o_t[:, :], full()).then_inc(s_bank_free, 1)
                if kind == "wo":
                    p = full()
                    ga = spread(gates[:, ds(b, 1), 0, :], 1, TU)
                    v.tensor_tensor(attn[:, :, :], p.rearrange("p (t d) -> p t d", t=TU), ga, ALU.mult) \
                        .then_inc(s_bank_free, 1)
                    dve.wait_ge(s_bank_free, use["base"] + use["n"])
                    link(v.tensor_tensor(res, res, attn[:, :, :], ALU.add), plain=True)
                if kind == "stat2":
                    dve.sem_inc(s_alone, 1)
                    for t in range(TU):
                        last = v.bn_stats(stats2[:, t, :], x_all[:, ds(b * TB + qb * TU + t, 1), :])
                    link(last, plain=True)
                    for t in range(TU):
                        last = v.bn_aggr(mean_var2[:, t, :], stats2[:, t, :])
                    link(last)
                if kind == "root2":
                    link(v.tensor_scalar(var_e2[:, :], mean_var2[:, :, 1], LN_EPS, None, ALU.add))
                if kind in ("root2", "root2 b", "root2 c"):
                    rsqrt(rstd2[:, :], var_e2[:, :], TU, kind == "root2")
                if kind == "xn2":
                    wait(dve, s_scattered, 16 * 2 * TU * unit)
                    for t in range(TU):
                        last = v.tensor_scalar(xn2[:, t, :], x_all[:, ds(b * TB + qb * TU + t, 1), :],
                                               mean_var2[:, t, 0:1], rstd2[:, t:t + 1], ALU.subtract, ALU.mult)
                    last.then_inc(s_xn2, 1)
                    dve.wait_ge(s_xn2, unit + 1)
                s, m, r, over, sg = (pick_f[:, i, :] for i in range(5))
                if kind == "pick":
                    first2 = [spread(mod_pick[:, ds(b, 1), i, :], 1, TU) for i in (1, 0)]
                    link(v.tensor_tensor(pick[:, :, :], xn2[:, :, 0:2], first2[0], ALU.mult))
                    link(v.tensor_tensor(pick[:, :, :], pick[:, :, :], first2[1], ALU.add))
                    link(v.tensor_tensor(s, pick[:, :, 0], pick[:, :, 1], ALU.add))
                    link(v.tensor_scalar(m, s, -1.0, None, ALU.mult))
                    link(v.tensor_tensor(m, m, s, ALU.max))
                    link(v.tensor_copy(pick_i[:, 0, :], m))
                    link(v.tensor_copy(r, pick_i[:, 0, :]))
                if kind == "pick2":
                    link(v.tensor_tensor(over, r, m, ALU.is_gt))
                    link(v.tensor_tensor(r, r, over, ALU.subtract))
                    link(v.tensor_scalar(sg, s, 0.0, 2.0, ALU.is_ge, ALU.mult))
                    link(v.scalar_tensor_tensor(out=r, in0=sg, scalar=-1.0, in1=r, op0=ALU.add, op1=ALU.mult))
                    link(v.tensor_copy(pick_i[:, 0, :], r))
                    link(v.tensor_scalar(pick_i[:, 1, :], pick_i[:, 0, :], NE - 1, None, ALU.bitwise_and))
                    h = spread(pick_i[:, 1, :].rearrange("p (t a) -> p t a", a=1), 2, NE)
                    link(v.tensor_tensor(near[:, :, :], expert[:, :, :], h, ALU.subtract))
                    link(v.tensor_scalar(near[:, :, :], near[:, :, :], NE - 1, None, ALU.bitwise_and))
                    v.tensor_scalar(w8[:, qb, :, :], near[:, :, :], 1.0, 0.5, ALU.is_le, ALU.mult).then_inc(s_w8, 1)
                if kind == "rank":
                    v.tensor_copy(rank[:, :, :, :].rearrange("p i t e -> p (i t e)"), full()[:, 0:2 * TU * NE]) \
                        .then_inc(s_bank_free, 1)
                    dve.wait_ge(s_bank_free, use["base"] + use["n"])
                    for t in range(1, TU):
                        link(v.tensor_tensor(rank[:, 1, t, :], rank[:, 1, t, :], rank[:, 1, t - 1, :], ALU.add))
                    link(v.tensor_tensor(rank[:, 0, 1:TU, :], rank[:, 0, 1:TU, :], rank[:, 1, 0:TU - 1, :], ALU.add))
                    link(v.tensor_scalar(n_steps_i[:, :], rank[:, 1, TU - 1, :], float(P - 1), None, ALU.add))
                    link(v.tensor_scalar(n_steps_i[:, :], n_steps_i[:, :], P.bit_length() - 1, None, ALU.logical_shift_right))
                    link(v.tensor_copy(n_steps[:, :], n_steps_i[:, :]))
                    each = spread(n_steps[:, :].rearrange("p (a e) -> p a e", a=1), 1, NE)
                    link(v.tensor_tensor(up_to_n[:, :, :], up_to[:, :, :], each, ALU.mult))
                    link(v.tensor_reduce(ends[:, :], up_to_n[:, :, :], AX.X, ALU.add))
                    link(v.tensor_tensor(starts[:, :], ends[:, :], n_steps[:, :], ALU.subtract))
                if kind == "place":
                    first = spread(starts[:, :].rearrange("p (a e) -> p a e", a=1), 1, TU)
                    link(v.scalar_tensor_tensor(out=rank[:, 0, :, :], in0=first, scalar=float(P), in1=rank[:, 0, :, :],
                                                op0=ALU.mult, op1=ALU.add))
                    for j in range(2):
                        last = v.scalar_tensor_tensor(out=place_of[:, j, :, :], in0=near[:, :, :], scalar=float(j),
                                                      in1=rank[:, 0, :, :], op0=ALU.is_equal, op1=ALU.mult)
                    link(last)
                    link(v.tensor_reduce(place_f[:, :, :].rearrange("p j t -> p (j t)"),
                                         place_of[:, :, :, :].rearrange("p j t e -> p (j t) e"), AX.X, ALU.add))
                    v.tensor_copy(place[:, qb, :, :], place_f[:, :, :]).then_inc(s_place, 1)
                if kind == "steps":
                    end = spread(ends[:, :].rearrange("p (a e) -> p a e", a=1), 1, QUARTERS * TU)
                    link(v.tensor_tensor(over_end[:, :, :], end, step_no[:, :, :], ALU.is_le))
                    link(v.tensor_reduce(of_step[:, :], over_end[:, :, :], AX.X, ALU.add))
                    link(v.tensor_scalar(of_step[:, :], of_step[:, :], float(NE - 1), float(P), ALU.min, ALU.mult))
                    v.tensor_scalar(w_row[:, qb, :], of_step[:, :], row_no[:, 0:1], None, ALU.add).then_inc(s_w_row, 1)
                if kind == "hsT":
                    q, w = which, quarter_steps(which) * P
                    p = full()
                    wait(dve, s_h1_used, STEPS * unit + ((q - 1) * TU if q >= 2 else (QUARTERS - 1) * TU - STEPS if q == 0 else 0))
                    v.tensor_scalar(h2_t[:, q % 2, 0:w], p[:, 0:w], mod_t[:, 4, ds(b, 1)], mod_t[:, 3, ds(b, 1)],
                                    ALU.mult, ALU.add).then_inc(s_bank_free, 1)
                    dve.sem_inc(s_turned, 1)
                y0, y1 = y_tok[:, 0, :, :], y_tok[:, 1, :, :]
                if kind == "sum":
                    dve.wait_ge(s_gathered, 16 * 2 * TU * (unit + 1))
                    link(v.tensor_tensor(y0, y0, y1, ALU.add))
                    gb = spread(gates[:, ds(b, 1), 1, :], 1, TU)
                    link(v.scalar_tensor_tensor(out=y0, in0=y0, scalar=0.5, in1=gb, op0=ALU.mult, op1=ALU.mult))
                    v.tensor_tensor(res, res, y0, ALU.add).then_inc(s_sum, 1)
                if kind == "last sum":
                    for t in range(TU):
                        dve.wait_ge(s_gathered_last[t], 32)
                        link(v.tensor_tensor(y0[:, t, :], y0[:, t, :], y1[:, t, :], ALU.add))
                        link(v.scalar_tensor_tensor(out=y0[:, t, :], in0=y0[:, t, :], scalar=0.5,
                                                    in1=gates[:, b, 1, :], op0=ALU.mult, op1=ALU.mult))
                        v.tensor_tensor(res[:, t, :], res[:, t, :], y0[:, t, :], ALU.add).then_inc(s_sum_last, 1)
                if kind == "ffn":
                    u, p = which, full()
                    if u < 2:
                        wait(dve, s_h1_used, STEPS * unit)
                    else:
                        dve.wait_ge(s_h1_used, STEPS * unit + u - 1)
                    for ch in range(NC):
                        last = v.tensor_scalar(h1[:, u % 2, ch, :], p[:, ch * P:(ch + 1) * P],
                                               w_ring[:, u % WRING, 2 * DFF + ch:2 * DFF + ch + 1], 0.0, ALU.add, ALU.max)
                    last.then_inc(s_bank_free, 1)
                    if u:
                        keep_y(unit, u - 1)
                if kind == "end":
                    keep_y(unit, STEPS - 1)

            def phase(b, qb, kind, i=0):
                begin(kind, qb, i)
                items = PLAN[kind, qb]
                before = (b, 0) if qb else (b - 1, 1)
                nkb = KB_OF[qb]
                for l in range(SLOTS_OF[qb]):
                    for item in items[l]:
                        if item[0] in PREP:
                            prep(item, b, qb)
                        else:
                            finish(item, b, qb)
                    ended, k = (l + 1 - LAG) % nkb == 0, (l + 1 - LAG) // nkb - 1
                    if ended and k >= 0:
                        evacuate(b, qb, k)
                    elif ended and k == -1 and (kind, qb) != ("first", 0):
                        evacuate(*before, NKV - 1)

            dve.wait_ge(s_x0, 16)
            for item in prep_items(0)[:PREP.index("lnT")]:
                prep(item, 0, 0)
            p = full()
            link(v.tensor_copy(mod_t[:, :, :], p[:, 0:6 * NB].rearrange("p (i b) -> p i b", b=NB)))
            for i in (1, 4):
                link(v.tensor_scalar(mod_t[:, i, :], mod_t[:, i, :], 1.0, None, ALU.add))
            v.tensor_copy(nw_a[:, 0:1], mod_t[:, 0, 0:1]).then_inc(s_bank_free, 1)
            for item in prep_items(0)[PREP.index("lnT"):]:
                prep(item, 0, 0)
            for b in range(NB):
                p = full()
                v.tensor_copy(gates[:, b, 0, :], p[:, 0:D])
                v.tensor_copy(gates[:, b, 1, :], p[:, 3 * D:4 * D])
                v.tensor_copy(mod_pick[:, b, 0, :], p[:, D:D + 2])
                v.tensor_scalar(mod_pick[:, b, 1, :], p[:, 2 * D:2 * D + 2], 1.0, None, ALU.add).then_inc(s_bank_free, 1)
                dve.wait_ge(s_bank_free, use["base"] + use["n"])
            for b in range(0, NB, 2):
                g = gates[:, b:b + 2, :, :].rearrange("p b i d -> p (b i d)")
                size = y_tok[:, 0, :, :].rearrange("p t d -> p (t d)")
                link(v.scalar_tensor_tensor(out=size, in0=g, scalar=-1.0, in1=g, op0=ALU.mult, op1=ALU.max))
                link(v.tensor_scalar(size, size, 0.25, None, ALU.max))
                link(v.tensor_scalar(g, g, 0.0, 2.0, ALU.is_ge, ALU.mult))
                link(v.scalar_tensor_tensor(out=g, in0=g, scalar=-1.0, in1=size, op0=ALU.add, op1=ALU.mult))
            dve.wait_ge(s_const, CONSTS)
            v.tensor_copy(step_no[:, :, :], step_i[:, :, :])
            link(v.tensor_copy(row_no[:, :], row_i[:, :]))
            dve.wait_ge(s_x, 16)
            phase(0, 0, "first")
            dve.wait_ge(s_h_zero, 32)
            phase(0, 1, "first")
            with dve.Fori(0, NB - 2) as i:
                dve.sem_clear(s_chain)
                chain["n"] = 0
                for qb in range(2):
                    phase(i + 1, qb, "mid", i)
            dve.sem_clear(s_chain)
            chain["n"] = 0
            for qb in range(2):
                phase(NB - 1, qb, "last")
            evacuate(NB - 1, 1, NKV - 1)
            begin("tail")
            for item in PLAN_TAIL:
                finish(item, NB, 0)


def rope_tables():
    inv = (np.float32(1.0) / np.float32(10000.0) ** (np.arange(0, HD, 2, dtype=np.float32) / np.float32(HD))).astype(np.float32)
    angle = np.outer(np.arange(SEQ, dtype=np.float32), inv).astype(np.float32)
    angle = np.concatenate([angle, angle], axis=-1)
    sign = np.where(np.arange(HD) < HD // 2, -1.0, 1.0).astype(np.float32)
    return np.stack([np.cos(angle), np.sin(angle) * sign]).astype(np.float32)


def kernel(**inputs):
    import concourse.bacc as bacc
    from concourse.bass_utils import run_bass_kernel_spmd

    nc = bacc.Bacc("TRN2", target_bir_lowering=False, num_devices=1)
    given = {n.removeprefix("L0_"): np.asarray(a) for n, a in inputs.items()}
    arrays = {
        "x": given["attn_x"],
        "wqkv": np.concatenate([given["attn_Wq"], given["attn_Wk"], given["attn_Wv"]]).T,
        "wo": given["attn_Wo"].T,
        "q_w": given["attn_q_norm_w"],
        "k_w": given["attn_k_norm_w"],
        "weights": np.concatenate([
            given["ffn_W1"],
            given["ffn_W2"].reshape(NE, NC, P, D).transpose(0, 2, 1, 3).reshape(NE, P, NC * D),
            given["ffn_b1"].reshape(NE, NC, P).transpose(0, 2, 1),
            np.broadcast_to(given["ffn_b2"][:, None, :], (NE, P, D))], axis=2).reshape(NE * P, WROW),
        "c": given["c"].T,
        "wmod": given["wmod"],
        "rope": rope_tables(),
    }
    arrays = {f"in_{n}": np.ascontiguousarray(a) for n, a in arrays.items()}
    args = [nc.dram_tensor(n, a.shape, mybir.dt.from_np(a.dtype), kind="ExternalInput").ap() for n, a in arrays.items()]
    args.append(nc.dram_tensor("out", (NB, SEQ, D), F32, kind="ExternalOutput").ap())
    adaln_block(nc, *args)
    r = run_bass_kernel_spmd(nc, [arrays], core_ids=[0])
    return r.results[0]["out"]
```
